# Optimizing a Trainium2 kernel written in Bass

```python
import numpy as np
import jax
import jax.numpy as jnp

def _softmax(x, axis=-1):
    return jax.nn.softmax(x, axis=axis)

def _gelu(x):
    return jax.nn.gelu(x, approximate=True)

def _silu(x):
    return jax.nn.silu(x)

def _sigmoid(x):
    return jax.nn.sigmoid(x)

def _layernorm(x, axis=-1, eps=1e-05):
    m = jnp.mean(x, axis=axis, keepdims=True)
    v = jnp.var(x, axis=axis, keepdims=True)
    return (x - m) / jnp.sqrt(v + eps)

def _scatter_add(tgt, idx, src, axis=0):
    return tgt.at[idx].add(src)

def _segment_sum(src, seg, n):
    return jax.ops.segment_sum(src, seg, n)
kernel_name = 'mk_macaron_d1_jaxref_r8_f5e803'

def setup_inputs(seed: int=0):
    np.random.seed(seed)
    _w = jnp.asarray

    def _L0_attn_setup():
        import jax, jax.numpy as jnp
        import numpy as np
        NUM_HEADS = 16
        EPS = float(jnp.finfo(jnp.float32).eps)

        def rms_norm(x, w):
            ms = jnp.mean(x * x, axis=-1, keepdims=True)
            return x * jax.lax.rsqrt(ms + EPS) * w
        key = jax.random.key(seed)
        k = jax.random.split(key, 5)
        B, N, D = (4, 256, 128)
        Dh = D // NUM_HEADS
        return {'x': jax.random.normal(k[0], (B, N, D), dtype=jnp.float32), 'Wq': jax.random.normal(k[1], (D, D), dtype=jnp.float32) * 0.02, 'Wk': jax.random.normal(k[2], (D, D), dtype=jnp.float32) * 0.02, 'Wv': jax.random.normal(k[3], (D, D), dtype=jnp.float32) * 0.02, 'Wo': jax.random.normal(k[4], (D, D), dtype=jnp.float32) * 0.02, 'qn_w': jnp.ones((Dh,), dtype=jnp.float32), 'kn_w': jnp.ones((Dh,), dtype=jnp.float32)}
    _L0_attn_in = _L0_attn_setup()

    def _L0_ffn_setup():
        import jax, jax.numpy as jnp
        import numpy as np
        K = 2
        key = jax.random.key(seed)
        ks = jax.random.split(key, 7)
        B, S, D, E = (2, 256, 128, 8)
        H = 4 * D
        sd = 1.0 / np.sqrt(D)
        sh = 1.0 / np.sqrt(H)
        return {'x': jax.random.normal(ks[0], (B, S, D), jnp.float32), 'Wr': jax.random.normal(ks[1], (D, E), jnp.float32) * sd, 'br': jax.random.normal(ks[2], (E,), jnp.float32) * sd, 'W1': jax.random.normal(ks[3], (E, D, H), jnp.float32) * sd, 'b1': jax.random.normal(ks[4], (E, H), jnp.float32) * sd, 'W2': jax.random.normal(ks[5], (E, H, D), jnp.float32) * sh, 'b2': jax.random.normal(ks[6], (E, D), jnp.float32) * sh}
    _L0_ffn_in = _L0_ffn_setup()
    _d = {'L0_attn_x': _L0_attn_in['x'], 'L0_attn_Wq': _L0_attn_in['Wq'], 'L0_attn_Wk': _L0_attn_in['Wk'], 'L0_attn_Wv': _L0_attn_in['Wv'], 'L0_attn_Wo': _L0_attn_in['Wo'], 'L0_attn_qn_w': _L0_attn_in['qn_w'], 'L0_attn_kn_w': _L0_attn_in['kn_w'], 'L0_ffn_Wr': _L0_ffn_in['Wr'], 'L0_ffn_br': _L0_ffn_in['br'], 'L0_ffn_W1': _L0_ffn_in['W1'], 'L0_ffn_b1': _L0_ffn_in['b1'], 'L0_ffn_W2': _L0_ffn_in['W2'], 'L0_ffn_b2': _L0_ffn_in['b2']}
    _x0 = _d['L0_attn_x']
    _d['L0_attn_x'] = jax.random.normal(jax.random.fold_in(jax.random.key(seed), 1), (4, 1024, 128), dtype=_x0.dtype)
    del _x0
    return _d

def reference(L0_attn_x, L0_attn_Wq, L0_attn_Wk, L0_attn_Wv, L0_attn_Wo, L0_attn_qn_w, L0_attn_kn_w, L0_ffn_Wr, L0_ffn_br, L0_ffn_W1, L0_ffn_b1, L0_ffn_W2, L0_ffn_b2):

    def _L0_attn_ref(x, Wq, Wk, Wv, Wo, qn_w, kn_w):
        import jax, jax.numpy as jnp
        import numpy as np
        NUM_HEADS = 16
        EPS = float(jnp.finfo(jnp.float32).eps)

        def rms_norm(x, w):
            ms = jnp.mean(x * x, axis=-1, keepdims=True)
            return x * jax.lax.rsqrt(ms + EPS) * w
        B, N, D = x.shape
        H = NUM_HEADS
        Dh = D // H
        scale = Dh ** (-0.5)

        def proj(W):
            return (x @ W.T).reshape(B, N, H, Dh).transpose(0, 2, 1, 3)
        q = rms_norm(proj(Wq), qn_w)
        k = rms_norm(proj(Wk), kn_w)
        v = proj(Wv)
        scores = jnp.einsum('bhnd,bhmd->bhnm', q, k) * scale
        attn = jax.nn.softmax(scores, axis=-1)
        out = jnp.einsum('bhnm,bhmd->bhnd', attn, v)
        out = out.transpose(0, 2, 1, 3).reshape(B, N, D)
        return out @ Wo.T

    def _L0_ffn_ref(x, Wr, br, W1, b1, W2, b2):
        import jax, jax.numpy as jnp
        import numpy as np
        K = 2
        E = Wr.shape[-1]
        scores = jnp.einsum('bsd,de->bse', x, Wr) + br
        _, topk_idx = jax.lax.top_k(scores, K)
        indicator = jax.nn.one_hot(topk_idx, E, dtype=scores.dtype).sum(-2)
        neg_inf = jnp.asarray(-jnp.inf, scores.dtype)
        weights = jax.nn.softmax(jnp.where(indicator > 0, scores, neg_inf), axis=-1)
        out = jnp.zeros_like(x)
        for i in range(E):
            xi = x * indicator[..., i:i + 1]
            h = jax.nn.relu(jnp.einsum('bsd,dh->bsh', xi, W1[i]) + b1[i])
            yi = jnp.einsum('bsh,hd->bsd', h, W2[i]) + b2[i]
            out = out + yi * weights[..., i:i + 1]
        return out
    x = L0_attn_x
    x = x + 0.5 * _L0_ffn_ref(_layernorm(x, axis=-1), L0_ffn_Wr, L0_ffn_br, L0_ffn_W1, L0_ffn_b1, L0_ffn_W2, L0_ffn_b2)
    x = x + _L0_attn_ref(_layernorm(x, axis=-1), L0_attn_Wq, L0_attn_Wk, L0_attn_Wv, L0_attn_Wo, L0_attn_qn_w, L0_attn_kn_w)
    x = x + 0.5 * _L0_ffn_ref(_layernorm(x, axis=-1), L0_ffn_Wr, L0_ffn_br, L0_ffn_W1, L0_ffn_b1, L0_ffn_W2, L0_ffn_b2)
    return x

_drawn_inputs = setup_inputs


def setup_inputs(seed=0):
    import zlib

    import numpy as np

    out = dict(_drawn_inputs(seed))
    spreads = {'L0_attn_qn_w': (1.0, 0.6), 'L0_attn_kn_w': (1.0, 0.6)}
    factors = {'L0_attn_Wq': 5.068, 'L0_attn_Wk': 4.381, 'L0_attn_Wv': 3.987, 'L0_attn_Wo': 4.207}
    for name, (base, spread) in spreads.items():
        noise = np.random.default_rng([zlib.crc32(name.encode()), seed]).standard_normal(out[name].shape)
        drawn = base * np.exp(spread * noise) if base else spread * noise
        out[name] = jnp.asarray(drawn.astype(out[name].dtype))
    for name, factor in factors.items():
        out[name] = (out[name] * factor).astype(out[name].dtype)
    return out
```

```python
from contextlib import ExitStack

import concourse.bass as bass
from concourse import mybir

F32 = mybir.dt.float32
BF16 = mybir.dt.bfloat16
I32 = mybir.dt.int32
ALU = mybir.AluOpType
ACT = mybir.ActivationFunctionType
AX = mybir.AxisListType

P = 128
BATCH, N, D = 4, 1024, 128
E, HID = 8, 512
HC = HID // P
TILES = BATCH * N // P
GROUPS = 2
GT = TILES // GROUPS
QUADS = GT // 4
ST = 256
SUB = ST // P
STILES = 2 * GT * P // ST + E
SROWS = STILES * ST
LOOPED = STILES // 4 - 2
W2_AT = HID
B1_AT = W2_AT + HC * D
B2_AT = B1_AT + HC
WUSED = B2_AT + 1
WSTEP = B2_AT + 4
EPS_LN = 1e-5
XSLOTS = 4
YSLOTS = 2
GSLOTS = 8
BIG = 3e38

HEADS = 16
DH = D // HEADS
SCALE = DH ** -0.5
EPS_RMS = 1.1920928955078125e-07
BT = N // P
PAIRS = HEADS // 2
SLOTS = 8
KROWS = SLOTS * DH
BLOCKS = 8
VW = 16
PSLOTS = 8
NB = BATCH * BLOCKS


MAX_BOUND = 60.0


class Plan:

    def __init__(self, items):
        self.items = items
        keys = [(kind, n) for block in items for kind, n, step in block if step is not None]
        self.event = {key: i for i, key in enumerate(keys)}
        self.bank = {key: 6 + i % 2 for i, key in enumerate(keys)}


def project(t):
    return [("turn_x", t, 0), ("qkv", t, 0), ("qkv", t + 1, 0), ("sums", t, None), ("sums", t + 1, None)]


def prepare(b):
    items = [x for t in range(b * BT, (b + 1) * BT, 2) for x in project(t)]
    items.append(("rsqrt", b, None))
    for t in range(b * BT, (b + 1) * BT):
        items += [("split", t, None), ("turn_q", t, 0), ("turn_k", t, 0)]
    return items


def fast_plan():
    plan = [[("norm", 0, None), ("norm", 1, None)] + prepare(0)]
    for K in range(NB + 4):
        b, k = divmod(K, BLOCKS)
        before = [("turn_o", K - 1, 3)] if 1 <= K <= NB else []
        out = (lambda a, c: ([("turn_a", K - 4, a)], [("wo", K - 4, c)]) if K >= 4 else ([], []))
        items = [("evac_o", K - 1, None)] if 1 <= K <= NB else []
        prep = K < NB and b + 1 < BATCH
        if prep and k < 4:
            t = BT * (b + 1) + 2 * k
            turn_a, wo = out(6, 7)
            items += before + [("turn_x", t, 4), ("qkv", t, 5), ("qkv", t + 1, 6)] + turn_a + wo
            items += [("sums", t, None), ("sums", t + 1, None)]
            if k == 3:
                items.append(("rsqrt", b + 1, None))
        elif prep:
            t = BT * (b + 1) + 2 * (k - 4)
            turn_a, wo = out(4, 6)
            items += [("split", t, None)] + before + [("split", t + 1, None)] + turn_a
            items += [("turn_q", t, 5), ("turn_k", t, 5)] + wo + [("turn_q", t + 1, 7), ("turn_k", t + 1, 7)]
        else:
            turn_a, wo = out(5, 6)
            items += before + turn_a + wo
        if k == 6 and b + 2 < BATCH:
            items.append(("norm", b + 2, None))
        plan.append(items)
    return plan


def general_plan():
    return [[("norm", b, None)] + prepare(b) + [("general", b, None)]
            + [x for t in range(b * BT, (b + 1) * BT) for x in (("turn_a", t, 0), ("wo", t, 0))]
            for b in range(BATCH)]


FAST, GENERAL = Plan(fast_plan()), Plan(general_plan())


class Link:

    def __init__(self, eng, sem, at=0):
        self.eng, self.sem, self.at = eng, sem, at

    def __call__(self, ins):
        ins.then_inc(self.sem, 1)
        self.at = self.at + 1
        self.eng.wait_ge(self.sem, self.at)


def build(nc, x_in, wq, wk, wv, wo, qn, kn, wr, br, w1, b1, w2, b2, out, PARTS=3):
    xs_dram = [nc.dram_tensor(f"sorted_x{g}", [SROWS, D], F32).ap() for g in range(GROUPS)]
    ys_dram = [nc.dram_tensor(f"sorted_y{g}", [SROWS, D], F32).ap() for g in range(GROUPS)]

    with ExitStack() as ctx:
        def sb(name, shape, dt=F32):
            return ctx.enter_context(nc.sbuf_tensor(name, shape, dt))

        def sem(name):
            return ctx.enter_context(nc.semaphore(name))

        psum = ctx.enter_context(nc.psum_tensor("psum", [P, 8, 512], F32))
        bank = [psum[:, i, :] for i in range(8)]

        ident = sb("ident", [P, P])
        ones = sb("ones", [P, P])
        before = sb("before", [P, P])
        erow_i = sb("erow_i", [P, E], I32)
        erow = sb("erow", [P, E])
        trow_i = sb("trow_i", [P, STILES], I32)
        trow = sb("trow", [P, STILES])
        wr_sb = sb("wr_sb", [P, E])
        br_sb = sb("br_sb", [P, E])
        bias_rows = sb("bias_rows", [E * HC + E, P])
        weights = sb("weights", [P, E * WSTEP])
        w_qkv = sb("w_qkv", [P, 3 * D])
        w_o = sb("w_o", [P, D])
        bias_cols = sb("bias_cols", [P, E * (HC + 1)])
        w_rows = sb("w_rows", [P, 4, D])
        w8 = sb("w8", [P, 3, DH])
        ident_b = sb("ident_b", [P, P], BF16)
        wview = weights[:, :].rearrange("p (e s) -> p e s", e=E)
        X = sb("X", [P, TILES, D])
        XN = sb("XN", [P, TILES, D])
        arena = sb("arena", [P, PSLOTS * 1024])
        at = [0]

        def carve(shape):
            n = 1
            for x in shape[1:]:
                n *= x
            view = arena[:, at[0]:at[0] + n]
            at[0] += n
            assert at[0] <= PSLOTS * 1024
            if len(shape) == 4:
                return view.rearrange("p (a b c) -> p a b c", a=shape[1], b=shape[2])
            return view.rearrange("p (a b) -> p a b", a=shape[1])

        probs = arena[:, :].rearrange("p (s n) -> p s n", s=PSLOTS)
        zeros = arena[:, 0:2048]

        stats = sb("stats", [P, GT, 6])
        mv = sb("mv", [P, GT, 2])
        rin = sb("rin", [P, GT])
        rout = sb("rout", [P, GT])
        rtmp = sb("rtmp", [P, GT])
        xt = sb("xt", [P, 2, 512])
        sc = sb("sc", [P, GT, E])
        eq = sb("eq", [P, GT, E])
        oh = [sb(f"oh{k}", [P, GT, E]) for k in range(2)]
        both = sb("both", [P, GT, E])
        s2 = sb("s2", [P, GT, E])
        mx = [sb(f"mx{k}", [P, GT]) for k in range(2)]
        fst = sb("fst", [P, GT])
        diff = sb("diff", [P, GT])
        e2 = sb("e2", [P, GT])
        den = sb("den", [P, GT])
        gate = [sb(f"gate{k}", [P, TILES]) for k in range(2)]
        scan = [sb(f"scan{k}", [P, GT, E]) for k in range(2)]
        total = sb("total", [P, GT, E])
        place = sb("place", [P, GT, E])
        cnt_i = sb("cnt_i", [P, 2, E], I32)
        cnt = sb("cnt", [P, 6, E])
        dst_f = sb("dst_f", [P, GT])
        dest = [sb(f"dest{k}", [P, TILES], I32) for k in range(2)]
        over = sb("over", [P, STILES, E])
        owner = sb("owner", [P, STILES])
        w_at = sb("w_at", [P, GROUPS, STILES], I32)

        xs = sb("xs", [P, XSLOTS, SUB, D])
        xst = carve([P, 2, ST])
        wbuf = carve([P, 2, WSTEP])
        hid = carve([P, 2, HC, ST])
        yt = carve([P, 2, ST])
        ys = sb("ys", [P, YSLOTS, SUB, D])
        gat = sb("gat", [P, GSLOTS, D])

        qk_even = weights[:, 0:2 * PAIRS * N // 2].bitcast(BF16).rearrange("p (s h n) -> p s h n", s=2, h=PAIRS)
        qk_odd = sb("qk_odd", [P, 2, PAIRS, N], BF16)
        qT = [qk_even[:, 0, :, :], qk_odd[:, 0, :, :]]
        kT = [qk_even[:, 1, :, :], qk_odd[:, 1, :, :]]
        V = sb("V", [P, 2, BT, HEADS, VW])
        xa = sb("xa", [P, 2 * P])
        qk = sb("qk", [P, BT, 2 * D])
        sq = sb("sq", [P, 2, 2 * D])
        ss = sb("ss", [P, BT, 2 * HEADS])
        rs = sb("rs", [P, BT, 2 * HEADS])
        rst = sb("rst", [P, BT, 2 * HEADS])
        qh = sb("qh", [P, 2, 2 * D])
        rest = sb("rest", [P, 2 * D])
        stack = sb("stack", [P, 2, 2, HEADS, SLOTS, DH], BF16)
        oT = sb("oT", [P, 2, 512])
        osum = sb("osum", [P, 4, 4])
        att = xt[:, :, :].rearrange("p h (t d) -> p h t d", t=4)
        aT = sb("aT", [P, P])

        att8 = xt[:, :, :].rearrange("p h (t d) -> p (h t) d", t=4)
        reach = sb("reach", [P, 1])
        unbounded = sb("unbounded", [P, 1], I32)
        g_p, g_pt = arena[:, 0:1024], arena[:, 1024:2048]
        g_k = arena[:, 2048:2560].bitcast(BF16)
        g_q = arena[:, 2560:2624].bitcast(BF16)
        g_v = arena[:, 2624:2624 + BT * 2 * VW].rearrange("p (c r v) -> p c r v", c=BT, r=2)
        g_max = arena[:, 3000:3001]

        bounded = sem("bounded")
        attended = sem("attended")
        pool_alink = sem("pool_alink")
        dve_alink = sem("dve_alink")
        rs_ready = sem("rs_ready")
        normalised = sem("normalised")
        g_ready = sem("g_ready")
        g_scores = sem("g_scores")
        g_maxed = sem("g_maxed")
        g_exp = sem("g_exp")
        g_turned = sem("g_turned")
        g_copied = sem("g_copied")
        g_out = sem("g_out")
        g_done = sem("g_done")
        xnorm = sem("xnorm")
        scores_full = sem("scores_full")
        exp_done = sem("exp_done")
        pv_done = sem("pv_done")
        ot_full = sem("ot_full")
        aux_full = sem("aux_full")
        aux_read = sem("aux_read")
        squared = sem("squared")
        summed = sem("summed")
        
        stacked = sem("stacked")
        w_turned = sem("w_turned")
        w_copied = sem("w_copied")
        a_loaded = sem("a_loaded")
        w_again = sem("w_again")
        x_loaded = sem("x_loaded")
        w_loaded = sem("w_loaded")
        b_loaded = sem("b_loaded")
        filled = sem("filled")
        consts = sem("consts")
        pool_link = sem("pool_link")
        dve_link = sem("dve_link")
        bias_t = sem("bias_t")
        bias_in = sem("bias_in")
        xn_ready = sem("xn_ready")
        xt_ps = sem("xt_ps")
        xt_full = sem("xt_full")
        router_done = sem("router_done")
        diff_ready = sem("diff_ready")
        gate_exp = sem("gate_exp")
        picks = sem("picks")
        counted = sem("counted")
        routed = sem("routed")
        scattered = [sem(f"scattered{g}") for g in range(GROUPS)]
        xs_in = [sem(f"xs_in{k}") for k in range(XSLOTS)]
        ys_out = [sem(f"ys_out{k}") for k in range(YSLOTS)]
        g_in = [sem(f"g_in{k}") for k in range(GSLOTS)]
        xs_turned = sem("xs_turned")
        xst_full = sem("xst_full")
        w_full = sem("w_full")
        h_full = sem("h_full")
        relu_done = sem("relu_done")
        y_full = sem("y_full")
        yt_full = sem("yt_full")
        o_full = sem("o_full")
        ys_full = sem("ys_full")
        combined = sem("combined")
        out_done = sem("out_done")

        LOADS_W = 3 + E

        block = ctx.enter_context(nc.Block())

        def branch(eng, attend):
            eng.wait_ge(bounded, 1)
            far = eng.value_load(unbounded[0:1, 0:1], min_val=0, max_val=1)
            with eng.If(far > 0):
                attend(GENERAL)
            with eng.Else():
                attend(FAST)

        def sorted_quads(eng, step):
            for t in range(4):
                step(t, t, t == 0, False)
            with eng.Fori(1, 1 + LOOPED) as q:
                for j in range(4):
                    step(q * 4 + j, j, False, False)
            for j in range(4):
                step(STILES - 4 + j, j, False, j == 3)

        @block.sync
        def _(sp):
            xv = x_in.rearrange("b (n p) d -> p (b n) d", p=P)
            for g in range(4):
                sp.dma_start(X[:, g * 8:g * 8 + 8, :], xv[:, g * 8:g * 8 + 8, :]).then_inc(x_loaded, 16)
            sp.dma_start(bias_rows[0:E * HC, :], b1.rearrange("e (c p) -> (e c) p", p=P)).then_inc(b_loaded, 16)
            sp.dma_start(bias_rows[E * HC:, :], b2).then_inc(b_loaded, 16)
            sp.dma_start(wr_sb[:, :], wr).then_inc(w_loaded, 16)
            sp.dma_start(br_sb[:, :], br.rearrange("(a e) -> a e", a=1).to_broadcast([P, E])).then_inc(w_loaded, 16)
            sp.wait_ge(consts, 6)
            for g in range(GROUPS):
                for k in range(SROWS // (P * 16)):
                    sp.dma_start(xs_dram[g][k * P * 16:(k + 1) * P * 16, :].rearrange("(n p) d -> p n d", p=P),
                                 zeros[:, :].rearrange("p (n d) -> p n d", d=D)).then_inc(filled, 16)
            for i, w in enumerate((wq, wk, wv, wo)):
                sp.dma_start(w_rows[:, i, :], w).then_inc(a_loaded, 16)
            for i, w in enumerate((qn, kn)):
                sp.dma_start(w8[:, i, :], w.rearrange("(a d) -> a d", a=1).to_broadcast([P, DH]))\
                    .then_inc(a_loaded, 16)

            def load_weights(sem):
                sp.dma_start(wview[:, :, 0:HID], w1.rearrange("e d h -> d e h")).then_inc(sem, 16)
                for e in range(E):
                    sp.dma_start(wview[:, e, W2_AT:B1_AT].rearrange("p (c d) -> p c d", c=HC),
                                 w2[e].rearrange("(c p) d -> p c d", p=P)).then_inc(sem, 16)

            load_weights(w_loaded)

            def experts(f, g):
                ph = GROUPS * f + g
                base = ph * STILES
                sp.wait_ge(scattered[g], 16 * 2 * GT * (f + 1))

                def load(t, slot):
                    sp.dma_start(xs[:, slot, :, :],
                                 xs_dram[g][bass.ds(t * ST, ST), :].rearrange("(j p) d -> p j d", p=P))\
                        .then_inc(xs_in[slot], 16)

                for t in range(XSLOTS - 1):
                    if ph:
                        sp.wait_ge(xs_turned, base)
                    load(t, t)

                def step(t, slot, first, last):
                    if not isinstance(t, int) or t + XSLOTS - 1 < STILES:
                        if not (ph == 0 and first):
                            sp.wait_ge(xs_turned, t + base)
                        load(t + XSLOTS - 1, (slot + XSLOTS - 1) % XSLOTS)
                    sp.wait_ge(ys_full, t + (base + 1))
                    sp.dma_start(ys_dram[g][bass.ds(t * ST, ST), :].rearrange("(j p) d -> p j d", p=P),
                                 ys[:, slot % YSLOTS, :, :]).then_inc(ys_out[slot % YSLOTS], 16)

                sorted_quads(sp, step)

            for g in range(GROUPS):
                experts(0, g)
            if PARTS > 1:
                def reload(pl):
                    if pl is FAST:
                        sp.wait_ge(pv_done, 8 * BLOCKS * (BATCH - 1))
                    else:
                        sp.wait_ge(attended, 1)
                    load_weights(w_again)

                branch(sp, reload)
            if PARTS == 3:
                for g in range(GROUPS):
                    experts(1, g)
            if 1:
                ov = out.rearrange("b (n p) d -> p (b n) d", p=P)
                sp.wait_ge(combined, TILES * (2 if PARTS == 3 else 1))
                if PARTS == 2:
                    sp.wait_ge(attended, 1)
                    sp.wait_ge(w_again, 16 * (1 + E))
                sp.dma_start(ov, X[:, :, :]).then_inc(out_done, 16)
                sp.wait_ge(out_done, 16)

        @block.gpsimd
        def _(pool):
            link = Link(pool, pool_link)
            pool.memset(zeros[:, :], 0.0).then_inc(consts, 1)
            pool.memset(ones[:, :], 1.0).then_inc(consts, 1)
            link(pool.memset(ident[:, :], 0.0))
            pool.affine_select(out=ident[:, :], in_=ident[:, :], compare_op=ALU.not_equal, fill=1.0, base=0,
                               pattern=[[-1, P]], channel_multiplier=1).then_inc(consts, 1)
            link(pool.memset(before[:, :], 0.0))
            pool.affine_select(out=before[:, :], in_=before[:, :], compare_op=ALU.is_ge, fill=1.0, base=0,
                               pattern=[[-1, P]], channel_multiplier=1).then_inc(consts, 1)
            pool.iota(erow_i[:, :], pattern=[[-1, E]], base=E, channel_multiplier=0)
            link(pool.iota(trow_i[:, :], pattern=[[1, STILES]], base=0, channel_multiplier=0))
            pool.tensor_copy(erow[:, :], erow_i[:, :])
            pool.tensor_copy(trow[:, :], trow_i[:, :]).then_inc(consts, 1)
            link(pool.memset(V[:, :, :, :, :], 0.0))
            pool.memset(V[:, :, :, :, DH:DH + 1], 1.0).then_inc(consts, 1)
            pool.wait_ge(filled, 16 * (GROUPS * SROWS // (P * 16)))

            def scatter(f, g):
                ph = GROUPS * f + g
                pool.wait_ge(routed, ph + 1)
                for i in range(g * GT, (g + 1) * GT):
                    for k in range(2):
                        pool.indirect_dma_start(xs_dram[g], bass.IndirectOffsetOnAxis(ap=dest[k][:, i:i + 1], axis=0),
                                                XN[:, i, :], None).then_inc(scattered[g], 16)

            def gather(f, g):
                ph = GROUPS * f + g
                for k in range(YSLOTS):
                    pool.wait_ge(ys_out[k], 16 * (STILES // YSLOTS) * (ph + 1))
                for i in range(GT):
                    for k in range(2):
                        n = 2 * (ph * GT + i) + k
                        if n >= GSLOTS:
                            pool.wait_ge(combined, (n - GSLOTS) // 2 + 1)
                        pool.indirect_dma_start(gat[:, n % GSLOTS, :], None, ys_dram[g],
                                                bass.IndirectOffsetOnAxis(ap=dest[k][:, g * GT + i:g * GT + i + 1],
                                                                          axis=0)).then_inc(g_in[n % GSLOTS], 16)

            alink = Link(pool, pool_alink)

            def square(pl, t):
                pool.wait_ge(aux_read, pl.event["qkv", t] + 1)
                if t >= 2:
                    pool.wait_ge(summed, t - 1)
                pool.tensor_tensor(sq[:, t % 2, :], qk[:, t % BT, :], qk[:, t % BT, :], ALU.mult).then_inc(squared, 1)

            def normalise(t):
                heads = qh[:, t % 2, :].rearrange("p (h d) -> p h d", d=DH)
                keys = heads[:, HEADS:, :]
                pool.wait_ge(rs_ready, t // BT + 1)
                if t >= 2:
                    pool.wait_ge(stacked, t - 1)
                alink(pool.tensor_tensor(heads, qk[:, t % BT, :].rearrange("p (h d) -> p h d", d=DH),
                                         rs[:, t % BT, :].unsqueeze(2).to_broadcast([P, 2 * HEADS, DH]), ALU.mult))
                pool.tensor_tensor(keys, keys, w8[:, 2, :].unsqueeze(1).to_broadcast([P, HEADS, DH]), ALU.mult)\
                    .then_inc(normalised, 1)

            def attend(pl):
                alink.at = 0
                for items in pl.items:
                    for kind, n, _ in items:
                        if kind == "sums":
                            square(pl, n)
                        elif kind == "split":
                            normalise(n)

            for g in range(GROUPS):
                scatter(0, g)
            for g in range(GROUPS):
                gather(0, g)
            if PARTS > 1:
                branch(pool, attend)
            if PARTS == 3:
                for g in range(GROUPS):
                    scatter(1, g)
                for g in range(GROUPS):
                    gather(1, g)

        @block.vector
        def _(dve):
            link = Link(dve, dve_link)
            alink = Link(dve, dve_alink)

            def rsqrt(dst, src, tmp, link=link):
                link(dve.tensor_scalar(tmp.bitcast(I32), src.bitcast(I32), 1, None, ALU.logical_shift_right))
                link(dve.tensor_scalar(dst.bitcast(I32), tmp.bitcast(I32), -1.0, float(0x5f3759df), ALU.mult, ALU.add))
                for _ in range(4):
                    link(dve.tensor_tensor(tmp, dst, dst, ALU.mult))
                    link(dve.scalar_tensor_tensor(out=tmp, in0=tmp, scalar=-0.5, in1=src, op0=ALU.mult, op1=ALU.mult))
                    link(dve.scalar_tensor_tensor(out=dst, in0=tmp, scalar=1.5, in1=dst, op0=ALU.add, op1=ALU.mult))

            def layer_norm(tiles, ready, link=link):
                n = len(tiles)
                for i, t in enumerate(tiles):
                    last = dve.bn_stats(stats[:, i, :], X[:, t, :])
                link(last)
                for i in range(n):
                    last = dve.bn_aggr(mv[:, i, :], stats[:, i, :])
                link(last)
                link(dve.tensor_scalar(rin[:, 0:n], mv[:, 0:n, 1], EPS_LN, None, ALU.add))
                rsqrt(rout[:, 0:n], rin[:, 0:n], rtmp[:, 0:n], link)
                for i, t in enumerate(tiles):
                    dve.tensor_scalar(XN[:, t, :], X[:, t, :], mv[:, i, 0:1], rout[:, i:i + 1],
                                      ALU.subtract, ALU.mult).then_inc(ready, 1)

            def wide(ap):
                return ap.unsqueeze(2).to_broadcast([P, GT, E])

            def route(f, g):
                ph = GROUPS * f + g
                if f:
                    dve.wait_ge(scattered[g], 16 * 2 * GT)
                layer_norm(range(g * GT, (g + 1) * GT), xn_ready)
                for q in range(QUADS):
                    n = ph * QUADS + q
                    dve.wait_ge(xt_ps, n + 1)
                    if n >= 2:
                        dve.wait_ge(router_done, n - 1)
                    dve.tensor_copy(xt[:, q % 2, :], bank[q % 2][:, :]).then_inc(xt_full, 1)
                dve.wait_ge(router_done, (ph + 1) * QUADS)
                scores = bank[2][:, 0:GT * E].rearrange("p (t e) -> p t e", e=E)
                link(dve.tensor_tensor(sc[:, :, :], scores, br_sb[:, :].unsqueeze(1).to_broadcast([P, GT, E]), ALU.add))
                for k, s in enumerate((sc, s2)):
                    link(dve.tensor_reduce(mx[k][:, :], s[:, :, :], AX.X, ALU.max))
                    link(dve.tensor_tensor(eq[:, :, :], s[:, :, :], wide(mx[k][:, :]), ALU.is_equal))
                    link(dve.tensor_tensor(eq[:, :, :], eq[:, :, :],
                                           erow[:, :].unsqueeze(1).to_broadcast([P, GT, E]), ALU.mult))
                    link(dve.tensor_reduce(fst[:, :], eq[:, :, :], AX.X, ALU.max))
                    link(dve.tensor_tensor(oh[k][:, :, :], eq[:, :, :], wide(fst[:, :]), ALU.is_equal))
                    if k == 0:
                        link(dve.scalar_tensor_tensor(out=s2[:, :, :], in0=oh[0][:, :, :], scalar=-BIG,
                                                      in1=sc[:, :, :], op0=ALU.mult, op1=ALU.add))
                dve.tensor_tensor(both[:, :, :], oh[0][:, :, :], oh[1][:, :, :], ALU.add).then_inc(picks, 1)
                dve.tensor_tensor(diff[:, :], mx[1][:, :], mx[0][:, :], ALU.subtract).then_inc(diff_ready, 1)
                dve.wait_ge(gate_exp, ph + 1)
                cols = slice(g * GT, (g + 1) * GT)
                link(dve.tensor_scalar(den[:, :], e2[:, :], 1.0, None, ALU.add))
                link(dve.reciprocal(fst[:, :], den[:, :]))
                link(dve.tensor_scalar(gate[0][:, cols], fst[:, :], 0.5, None, ALU.mult))
                link(dve.tensor_tensor(gate[1][:, cols], gate[0][:, cols], e2[:, :], ALU.mult))
                dve.wait_ge(counted, ph + 1)
                within = bank[3][:, 0:GT * E].rearrange("p (t e) -> p t e", e=E)
                totals = bank[3][:, GT * E:2 * GT * E].rearrange("p (t e) -> p t e", e=E)
                link(dve.tensor_copy(total[:, :, :], totals))
                src, s, k = total, 1, 0
                while s < GT:
                    dve.tensor_copy(scan[k][:, 0:s, :], src[:, 0:s, :])
                    link(dve.tensor_tensor(scan[k][:, s:GT, :], src[:, s:GT, :], src[:, 0:GT - s, :], ALU.add))
                    src, s, k = scan[k], 2 * s, 1 - k
                dve.tensor_tensor(place[:, :, :], src[:, :, :], total[:, :, :], ALU.subtract)
                link(dve.tensor_scalar(cnt_i[:, 0, :], src[:, GT - 1, :], float(ST - 1), None, ALU.add))
                link(dve.tensor_scalar(cnt_i[:, 1, :], cnt_i[:, 0, :], ST.bit_length() - 1, None,
                                       ALU.logical_shift_right))
                link(dve.tensor_copy(cnt[:, 0, :], cnt_i[:, 1, :]))
                for n, s in enumerate((1, 2, 4)):
                    dve.tensor_copy(cnt[:, n + 1, 0:s], cnt[:, n, 0:s])
                    link(dve.tensor_tensor(cnt[:, n + 1, s:E], cnt[:, n, s:E], cnt[:, n, 0:E - s], ALU.add))
                link(dve.tensor_tensor(cnt[:, 4, :], cnt[:, 3, :], cnt[:, 0, :], ALU.subtract))
                link(dve.tensor_scalar(cnt[:, 5, :], cnt[:, 4, :], float(ST), None, ALU.mult))
                link(dve.tensor_tensor(place[:, :, :], place[:, :, :], within, ALU.add))
                link(dve.tensor_tensor(place[:, :, :], place[:, :, :],
                                       cnt[:, 5, :].unsqueeze(1).to_broadcast([P, GT, E]), ALU.add))
                for k in range(2):
                    link(dve.tensor_tensor(eq[:, :, :], oh[k][:, :, :], place[:, :, :], ALU.mult))
                    link(dve.tensor_reduce(dst_f[:, :], eq[:, :, :], AX.X, ALU.add))
                    link(dve.tensor_copy(dest[k][:, cols], dst_f[:, :]))
                link(dve.tensor_tensor(over[:, :, :], cnt[:, 3, :].unsqueeze(1).to_broadcast([P, STILES, E]),
                                       trow[:, :].unsqueeze(2).to_broadcast([P, STILES, E]), ALU.is_le))
                link(dve.tensor_reduce(owner[:, :], over[:, :, :], AX.X, ALU.add))
                dve.tensor_scalar(w_at[:, g, :], owner[:, :], float(E - 1), float(WSTEP), ALU.min, ALU.mult)\
                    .then_inc(routed, 1)

            def experts(f, g, between):
                ph = GROUPS * f + g
                base = ph * STILES

                def turned(t, slot):
                    dve.wait_ge(xs_turned, t + (base + 1))
                    dve.tensor_copy(xst[:, slot % 2, :], bank[4][:, 0:ST]).then_inc(xst_full, 1)

                def rows(t, slot):
                    dve.wait_ge(o_full, t + (base + 1))
                    if not isinstance(t, int) or t >= YSLOTS:
                        dve.wait_ge(ys_out[slot % 2], (t - slot % 2) * 8 + 16 * (STILES // 2) * ph)
                    elif ph:
                        dve.wait_ge(ys_out[slot % 2], 16 * (STILES // 2) * ph)
                    dve.tensor_copy(ys[:, slot % 2, :, :], bank[5][:, 0:ST].rearrange("p (j d) -> p j d", d=D))\
                        .then_inc(ys_full, 1)

                turned(0, 0)

                def step(t, slot, first, last):
                    if not last:
                        turned(t + 1, slot + 1)
                    if not first:
                        rows(t - 1, slot - 1 + 4)

                sorted_quads(dve, step)
                rows(STILES - 1, 3)

            def combine(f, g):
                ph = GROUPS * f + g
                for i in range(GT):
                    for k in range(2):
                        n = 2 * (ph * GT + i) + k
                        t = g * GT + i
                        dve.wait_ge(g_in[n % GSLOTS], 16 * (n // GSLOTS + 1))
                        ins = dve.scalar_tensor_tensor(out=X[:, t, :], in0=gat[:, n % GSLOTS, :],
                                                       scalar=gate[k][:, t:t + 1], in1=X[:, t, :],
                                                       op0=ALU.mult, op1=ALU.add)
                        if k == 0:
                            link(ins)
                        else:
                            ins.then_inc(combined, 1)

            def place_biases():
                dve.tensor_copy(wview[:, :, B1_AT:B2_AT], bias_cols[:, 0:E * HC].rearrange("p (e c) -> p e c", e=E))
                dve.tensor_copy(wview[:, :, B2_AT], bias_cols[:, E * HC:]).then_inc(bias_in, 1)

            def evac_o(pl, K):
                dve.wait_ge(pv_done, 8 * (K + 1))
                if K >= 2:
                    dve.wait_ge(aux_full, pl.event["turn_o", K - 2] + 1)
                dve.tensor_copy(oT[:, K % 2, :], bank[4 + K % 2]).then_inc(ot_full, 1)

            def norm(b):
                layer_norm(range(b * BT, (b + 1) * BT), xnorm, alink)

            def sums(t):
                dve.wait_ge(squared, t + 1)
                dve.tensor_reduce(ss[:, t % BT, :], sq[:, t % 2, :].rearrange("p (h d) -> p h d", d=DH),
                                  AX.X, ALU.add).then_inc(summed, 1)

            def rsqrt_qk(b):
                dve.wait_ge(summed, (b + 1) * BT)
                alink(dve.tensor_scalar(ss[:, :, :], ss[:, :, :], 1.0 / DH, EPS_RMS, ALU.mult, ALU.add))
                rsqrt(*(a[:, :, :].rearrange("p t h -> p (t h)") for a in (rs, ss, rst)), alink)
                dve.sem_inc(rs_ready, 1)

            def split(pl, t):
                u = t % 2
                dve.wait_ge(normalised, t + 1)
                if t >= 2:
                    dve.wait_ge(aux_full, pl.event["turn_k", t - 2] + 1)
                whole = qh[:, u, :].rearrange("p (a h d) -> p a h d", a=2, d=DH)
                left = rest[:, :].rearrange("p (a h d) -> p a h d", a=2, d=DH)
                first = [stack[:, u, a, :, 0, :] for a in range(2)]
                second = [stack[:, u, 0, :, 3, :], stack[:, u, 1, :, 1, :]]

                def wide(ap, n):
                    return ap.unsqueeze(2).to_broadcast([P, HEADS, n, DH])

                dve.tensor_copy(stack[:, u, 0, :, 0:3, :], wide(whole[:, 0], 3))
                alink(dve.tensor_copy(stack[:, u, 1, :, 0:SLOTS:3, :], wide(whole[:, 1], 3)))
                for a in range(2):
                    last = dve.tensor_tensor(left[:, a], whole[:, a], first[a], ALU.subtract)
                alink(last)
                dve.tensor_copy(stack[:, u, 0, :, 3:6, :], wide(left[:, 0], 3))
                alink(dve.tensor_copy(stack[:, u, 1, :, 1:SLOTS:3, :], wide(left[:, 1], 3)))
                dve.tensor_tensor(stack[:, u, 0, :, 6:8, :], wide(left[:, 0], 2), wide(second[0], 2), ALU.subtract)
                dve.tensor_tensor(stack[:, u, 1, :, 2:SLOTS:3, :], wide(left[:, 1], 2), wide(second[1], 2),
                                  ALU.subtract).then_inc(stacked, 1)

            def empty(pl, kind, n):
                src = bank[pl.bank[kind, n]]
                dve.wait_ge(aux_full, pl.event[kind, n] + 1)
                if kind == "turn_x":
                    ins = dve.tensor_copy(xa[:, :], src[:, 0:2 * P])
                elif kind == "qkv":
                    dve.tensor_copy(qk[:, n % BT, :], src[:, 0:2 * D])
                    ins = dve.tensor_copy(V[:, n // BT % 2, n % BT, :, 0:DH],
                                          src[:, 2 * D:3 * D].rearrange("p (h d) -> p h d", d=DH))
                elif kind in ("turn_q", "turn_k"):
                    to = (qT if kind == "turn_q" else kT)[n // BT % 2]
                    ins = dve.tensor_copy(to[:, :, n % BT * P:(n % BT + 1) * P],
                                          src.bitcast(BF16).rearrange("p (h n) -> p h n", h=PAIRS))
                elif kind == "turn_o":
                    half, g = divmod(n, 4)
                    v = src.rearrange("p (t j r) -> p t j r", t=4, j=4)
                    alink(dve.reciprocal(osum[:, :, :], v[:, :, :, DH]))
                    ins = dve.tensor_tensor(
                        att[:, half % 2, :, g * 4 * DH:(g + 1) * 4 * DH].rearrange("p t (j d) -> p t j d", d=DH),
                        v[:, :, :, 0:DH], osum[:, :, :].unsqueeze(3).to_broadcast([P, 4, 4, DH]), ALU.mult)
                elif kind == "turn_a":
                    ins = dve.tensor_copy(aT[:, :], src[:, 0:P])
                elif kind == "wo":
                    ins = dve.tensor_tensor(X[:, n, :], src[:, 0:D], X[:, n, :], ALU.add)
                ins.then_inc(aux_read, 1)

            def general(pl, b):
                links, base = 5, alink.at
                dve.wait_ge(aux_read, pl.event["turn_k", (b + 1) * BT - 1] + 1)
                with dve.Fori(0, PAIRS) as pair:
                    with dve.Fori(0, BT) as i:
                        turn = pair * BT + i
                        at = (turn + b * PAIRS * BT) * 2
                        alink.at = turn * links + base
                        dve.tensor_copy(g_k, kT[b % 2][:, bass.ds(pair, 1), :].rearrange("p a n -> p (a n)"))
                        for r in range(2):
                            dve.tensor_copy(g_v[:, :, r, :],
                                            V[:, b % 2, :, bass.ds(pair * 2 + r, 1), :].rearrange("p c a v -> p c (a v)"))
                        alink(dve.tensor_copy(g_q, qT[b % 2][:, bass.ds(pair, 1), bass.ds(i * P, P)]
                                              .rearrange("p a n -> p (a n)")))
                        dve.sem_inc(g_ready, 1)
                        for r in range(2):
                            dve.wait_ge(g_scores, at + (r + 1))
                            dve.tensor_reduce(g_max, psum[:, 0:2, :].rearrange("p b n -> p (b n)"), AX.X, ALU.max,
                                              negate=True).then_inc(g_maxed, 1)
                            dve.wait_ge(g_turned, at + (r + 1))
                            dve.tensor_copy(g_pt, psum[:, 2:4, :].rearrange("p b n -> p (b n)")).then_inc(g_copied, 1)
                            dve.wait_ge(g_out, at + (r + 1))
                            alink(dve.reciprocal(osum[:, 0, 0:1], bank[4][:, DH:DH + 1]))
                            alink(dve.tensor_scalar(
                                att8[:, bass.ds(i, 1), bass.ds(pair * (2 * DH) + r * DH, DH)]
                                .rearrange("p a n -> p (a n)"),
                                bank[4][:, 0:DH], osum[:, 0, 0:1], None, ALU.mult))
                alink.at = base + PAIRS * BT * links
                dve.sem_inc(g_done, 1)

            def attend(pl):
                alink.at = 0
                dve.wait_ge(w_full, GROUPS * STILES)
                for items in pl.items:
                    for kind, n, step in items:
                        if step is not None:
                            empty(pl, kind, n)
                        elif kind == "evac_o":
                            evac_o(pl, n)
                        elif kind == "norm":
                            norm(n)
                        elif kind == "sums":
                            sums(n)
                        elif kind == "rsqrt":
                            rsqrt_qk(n)
                        elif kind == "split":
                            split(pl, n)
                        elif kind == "general":
                            general(pl, n)
                dve.wait_ge(aux_read, len(pl.event))
                dve.sem_inc(attended, 1)

            dve.memset(psum[:, 4:6, :], 0.0)
            dve.wait_ge(a_loaded, 16 * 6)
            dve.wait_ge(consts, 6)
            dve.tensor_copy(ident_b[:, :], ident[:, :])
            link(dve.tensor_tensor(w8[:, 2, :], w8[:, 0, :], w8[:, 1, :], ALU.mult))
            link(dve.tensor_scalar(w8[:, 2, :], w8[:, 2, :], SCALE, None, ALU.mult))
            link(dve.tensor_reduce(reach[:, :], w8[:, 2, :], AX.X, ALU.max, apply_absolute_value=True))
            dve.tensor_scalar(unbounded[:, :], reach[:, :], MAX_BOUND / DH, None, ALU.is_gt).then_inc(bounded, 1)
            dve.wait_ge(w_turned, 1)
            dve.tensor_copy(w_qkv[:, :], bank[6][:, 0:3 * D])
            dve.tensor_copy(w_o[:, :], bank[6][:, 3 * D:4 * D]).then_inc(w_copied, 1)
            dve.wait_ge(x_loaded, 64)
            dve.wait_ge(w_loaded, 16 * LOADS_W)
            dve.wait_ge(consts, 6)
            dve.wait_ge(bias_t, 1)
            link(dve.tensor_copy(bias_cols[:, :], bank[7][:, 0:E * (HC + 1)]))
            place_biases()
            for g in range(GROUPS):
                route(0, g)
            for g in range(GROUPS):
                experts(0, g, None)
            for g in range(GROUPS):
                combine(0, g)
            if PARTS > 1:
                branch(dve, attend)
            if PARTS == 3:
                dve.wait_ge(w_again, 16 * (1 + E))
                place_biases()
                for g in range(GROUPS):
                    route(1, g)
                for g in range(GROUPS):
                    experts(1, g, None)
                for g in range(GROUPS):
                    combine(1, g)

        @block.scalar
        def _(act):
            def route(f, g):
                ph = GROUPS * f + g
                act.wait_ge(diff_ready, ph + 1)
                act.activation(e2[:, :], diff[:, :], ACT.Exp).then_inc(gate_exp, 1)

            def experts(f, g):
                ph = GROUPS * f + g
                base = ph * STILES

                def fetch(t, slot):
                    at = act.value_load(w_at[0:1, g, bass.ds(t, 1)], min_val=0, max_val=(E - 1) * WSTEP)
                    if not (ph == 0 and isinstance(t, int) and t < 2):
                        act.wait_ge(yt_full, t + (base - 1))
                    act.activation(wbuf[:, slot % 2, 0:WUSED], weights[:, bass.ds(at, WUSED)], ACT.Copy)\
                        .then_inc(w_full, 1)

                act.wait_ge(routed, ph + 1)
                fetch(0, 0)

                def step(t, slot, first, last):
                    for c in range(HC):
                        act.wait_ge(h_full, t * HC + (base * HC + c + 1))
                        act.activation(hid[:, slot % 2, c, :], bank[c][:, 0:ST], ACT.Relu,
                                       bias=wbuf[:, slot % 2, B1_AT + c:B1_AT + c + 1]).then_inc(relu_done, 1)
                    if not last:
                        fetch(t + 1, slot + 1)
                    act.wait_ge(y_full, t + (base + 1))
                    act.activation(yt[:, slot % 2, :], bank[6][:, 0:ST], ACT.Identity,
                                   bias=wbuf[:, slot % 2, B2_AT:B2_AT + 1]).then_inc(yt_full, 1)

                sorted_quads(act, step)

            def attend(pl):
                if pl is GENERAL:
                    with act.Fori(0, NB * 2 * BT) as n:
                        act.wait_ge(g_maxed, n + 1)
                        act.activation(g_p, psum[:, 0:2, :].rearrange("p b n -> p (b n)"), ACT.Exp,
                                       bias=g_max).then_inc(g_exp, 1)
                    return

                def block(K):
                    for u in range(16):
                        act.wait_ge(scores_full, K * 16 + (u + 1))
                        if u >= PSLOTS or not isinstance(K, int):
                            act.wait_ge(pv_done, K * 8 + (u // 2 + 1 - PSLOTS // 2))
                        act.activation(probs[:, u % PSLOTS, :],
                                       psum[:, 2 * (u % 2):2 * (u % 2) + 2, :].rearrange("p b n -> p (b n)"),
                                       ACT.Exp).then_inc(exp_done, 1)

                block(0)
                with act.Fori(1, NB) as K:
                    block(K)

            act.wait_ge(w_loaded, 16 * LOADS_W)
            act.wait_ge(bias_in, 1)
            for g in range(GROUPS):
                route(0, g)
            for g in range(GROUPS):
                experts(0, g)
            if PARTS > 1:
                branch(act, attend)
            if PARTS == 3:
                act.wait_ge(bias_in, 2)
                for g in range(GROUPS):
                    route(1, g)
                for g in range(GROUPS):
                    experts(1, g)

        @block.tensor
        def _(pe):
            def route(f, g):
                ph = GROUPS * f + g

                def turn(q):
                    n = ph * QUADS + q
                    if n >= 2:
                        pe.wait_ge(xt_full, n - 1)
                    for j in range(4):
                        pe.wait_ge(xn_ready, ph * GT + 4 * q + j + 1)
                        mm = pe.transpose(bank[q % 2][:, j * P:(j + 1) * P], XN[:, g * GT + 4 * q + j, :], ident[:, :])
                    mm.then_inc(xt_ps, 1)

                turn(0)
                for q in range(QUADS):
                    if q + 1 < QUADS:
                        turn(q + 1)
                    n = ph * QUADS + q
                    pe.wait_ge(xt_full, n + 1)
                    for j in range(4):
                        at = (4 * q + j) * E
                        mm = pe.matmul(bank[2][:, at:at + E], xt[:, q % 2, j * P:(j + 1) * P], wr_sb[:, :],
                                       start=True, stop=True)
                    mm.then_inc(router_done, 1)
                pe.wait_ge(picks, ph + 1)
                flat = both[:, :, :].rearrange("p t e -> p (t e)")
                pe.matmul(bank[3][:, 0:GT * E], before[:, :], flat, start=True, stop=True)
                pe.matmul(bank[3][:, GT * E:2 * GT * E], ones[:, :], flat, start=True, stop=True)\
                    .then_inc(counted, 1)

            def experts(f, g):
                ph = GROUPS * f + g
                base = ph * STILES

                def turn(t, slot, first=False):
                    pe.wait_ge(xs_in[slot % XSLOTS], (t - slot % XSLOTS) * 4 + 16 * (STILES // 4 * ph + 1))
                    if not (ph == 0 and first):
                        pe.wait_ge(xst_full, t + base)
                    for j in range(SUB):
                        mm = pe.transpose(bank[4][:, j * P:(j + 1) * P], xs[:, slot % XSLOTS, j, :], ident[:, :])
                    mm.then_inc(xs_turned, 1)

                def back(t, slot, first=False):
                    pe.wait_ge(yt_full, t + (base + 1))
                    if not (ph == 0 and first):
                        pe.wait_ge(ys_full, t + base)
                    for j in range(SUB):
                        mm = pe.transpose(bank[5][:, j * P:(j + 1) * P], yt[:, slot % 2, j * P:(j + 1) * P],
                                          ident[:, :])
                    mm.then_inc(o_full, 1)

                turn(0, 0, True)

                def step(t, slot, first, last):
                    if not last:
                        turn(t + 1, slot + 1)
                    pe.wait_ge(xst_full, t + (base + 1))
                    pe.wait_ge(w_full, t + (base + 1))
                    for c in range(HC):
                        pe.matmul(bank[c][:, 0:ST], wbuf[:, slot % 2, c * P:(c + 1) * P], xst[:, slot % 2, :],
                                  start=True, stop=True).then_inc(h_full, 1)
                    if not first:
                        back(t - 1, slot - 1 + 4, isinstance(t, int) and t == 1)
                    for c in range(HC):
                        pe.wait_ge(relu_done, t * HC + (base * HC + c + 1))
                        mm = pe.matmul(bank[6][:, 0:ST], wbuf[:, slot % 2, W2_AT + c * D:W2_AT + (c + 1) * D],
                                       hid[:, slot % 2, c, :], start=(c == 0), stop=(c == HC - 1))
                    mm.then_inc(y_full, 1)

                sorted_quads(pe, step)
                back(STILES - 1, 3)

            def fill(pl, kind, n):
                i = pl.event[kind, n]
                dst = bank[pl.bank[kind, n]]
                if i >= 2:
                    pe.wait_ge(aux_read, i - 1)
                if kind == "turn_x":
                    for j in range(2):
                        pe.wait_ge(xnorm, n + j + 1)
                        mm = pe.transpose(dst[:, j * P:(j + 1) * P], XN[:, n + j, :], ident[:, :])
                elif kind == "qkv":
                    pe.wait_ge(aux_read, pl.event["turn_x", n - n % 2] + 1)
                    mm = pe.matmul(dst[:, 0:3 * D], xa[:, n % 2 * P:(n % 2 + 1) * P], w_qkv[:, :],
                                   start=True, stop=True)
                elif kind in ("turn_q", "turn_k"):
                    pe.wait_ge(stacked, n + 1)
                    flat = stack[:, n % 2, int(kind == "turn_k"), :, :, :].rearrange("p h s d -> p (h s d)")
                    for j in range(PAIRS):
                        mm = pe.transpose(dst.bitcast(BF16)[:, j * P:(j + 1) * P], flat[:, j * P:(j + 1) * P],
                                          ident_b[:, :])
                elif kind == "turn_o":
                    pe.wait_ge(ot_full, n + 1)
                    for j in range(4):
                        mm = pe.transpose(dst[:, j * P:(j + 1) * P], oT[:, n % 2, j * P:(j + 1) * P], ident[:, :])
                elif kind == "turn_a":
                    if pl is FAST:
                        pe.wait_ge(aux_read, pl.event["turn_o", n - n % 4 + 3] + 1)
                    else:
                        pe.wait_ge(g_done, n // BT + 1)
                    mm = pe.transpose(dst[:, 0:P], att8[:, n % 8, :], ident[:, :])
                elif kind == "wo":
                    pe.wait_ge(aux_read, pl.event["turn_a", n] + 1)
                    mm = pe.matmul(dst[:, 0:D], aT[:, :], w_o[:, :], start=True, stop=True)
                mm.then_inc(aux_full, 1)

            def scores(K, c, a):
                b, k = divmod(K, BLOCKS)
                half, g = divmod(k, 4)
                u = 16 * K + 2 * c + a
                pair = 2 * g + a
                if u >= 2:
                    pe.wait_ge(exp_done, u - 1)
                for r in range(2):
                    rows = slice(r * KROWS, (r + 1) * KROWS)
                    mm = pe.matmul(bank[2 * a + r], kT[b % 2][rows, pair, c * P:(c + 1) * P],
                                   qT[b % 2][rows, pair, half * 512:(half + 1) * 512], start=True, stop=True)
                mm.then_inc(scores_full, 1)

            def values(K, c):
                b, k = divmod(K, BLOCKS)
                g = k % 4
                if c == 0 and K >= 2:
                    pe.wait_ge(ot_full, K - 1)
                pe.wait_ge(exp_done, 16 * K + 2 * c + 2)
                for j in range(4):
                    u = 2 * c + j // 2
                    mm = pe.matmul(bank[4 + K % 2][32 * j:32 * j + VW, :], V[:, b % 2, c, 4 * g + j, :],
                                   probs[:, u % PSLOTS, j % 2 * 512:(j % 2 + 1) * 512],
                                   start=(c == 0), stop=(c == BT - 1))
                mm.then_inc(pv_done, 1)

            def fills(pl, block, at=None):
                for kind, n, step in block:
                    if step is not None and (at is None or step == at):
                        fill(pl, kind, n)

            def general(b):
                with pe.Fori(0, PAIRS * BT) as i:
                    turn = i + b * PAIRS * BT
                    pe.wait_ge(g_ready, turn + 1)
                    for r in range(2):
                        n = turn * 2 + (r + 1)
                        rows = slice(r * KROWS, (r + 1) * KROWS)
                        for h in range(2):
                            mm = pe.matmul(bank[h], g_q[rows, :], g_k[rows, h * 512:(h + 1) * 512],
                                           start=True, stop=True)
                        mm.then_inc(g_scores, 1)
                        pe.wait_ge(g_exp, n)
                        for c in range(BT):
                            mm = pe.transpose(bank[2 + c // 4][:, c % 4 * P:(c % 4 + 1) * P],
                                              g_p[:, c * P:(c + 1) * P], ident[:, :])
                        mm.then_inc(g_turned, 1)
                        pe.wait_ge(g_copied, n)
                        for c in range(BT):
                            mm = pe.matmul(bank[4][:, 0:VW], g_pt[:, c * P:(c + 1) * P], g_v[:, c, r, :],
                                           start=(c == 0), stop=(c == BT - 1))
                        mm.then_inc(g_out, 1)

            def attend(pl):
                if pl is GENERAL:
                    for items in pl.items:
                        for kind, n, step in items:
                            if kind == "general":
                                general(n)
                            elif step is not None:
                                fill(pl, kind, n)
                    return
                fills(pl, pl.items[0])
                LAG = 2
                for K in range(NB):
                    k = K % BLOCKS
                    if k == 0:
                        pe.wait_ge(aux_read, pl.event["turn_k", (K // BLOCKS + 1) * BT - 1] + 1)
                    for c in range(BT):
                        scores(K, c, 0)
                        s = 8 * k + c - LAG
                        if s >= 0:
                            values(K - k + s // 8, s % 8)
                        scores(K, c, 1)
                        fills(pl, pl.items[K + 1], c)
                    if k == BLOCKS - 1:
                        for c in range(BT - LAG, BT):
                            values(K, c)
                for K in range(NB, NB + 4):
                    fills(pl, pl.items[K + 1])

            pe.wait_ge(consts, 6)
            pe.wait_ge(a_loaded, 16 * 6)
            for i in range(4):
                mm = pe.transpose(bank[6][:, i * D:(i + 1) * D], w_rows[:, i, :], ident[:, :])
            mm.then_inc(w_turned, 1)
            pe.wait_ge(b_loaded, 32)
            pe.transpose(bank[7][:, 0:E * HC + E], bias_rows[:, :], ident[0:E * HC + E, 0:E * HC + E])\
                .then_inc(bias_t, 1)
            pe.wait_ge(w_loaded, 16 * LOADS_W)
            for g in range(GROUPS):
                route(0, g)
            pe.wait_ge(routed, 2)
            for g in range(GROUPS):
                experts(0, g)
            if PARTS > 1:
                pe.wait_ge(w_copied, 1)
                branch(pe, attend)
            if PARTS == 3:
                for g in range(GROUPS):
                    route(1, g)
                pe.wait_ge(routed, 4)
                for g in range(GROUPS):
                    experts(1, g)


_INS = ['L0_attn_x', 'L0_attn_Wq', 'L0_attn_Wk', 'L0_attn_Wv', 'L0_attn_Wo', 'L0_attn_qn_w', 'L0_attn_kn_w',
        'L0_ffn_Wr', 'L0_ffn_br', 'L0_ffn_W1', 'L0_ffn_b1', 'L0_ffn_W2', 'L0_ffn_b2']


def kernel(**inputs):
    import numpy as _np
    import concourse.bacc as _bacc
    from concourse import mybir as _mybir
    from concourse.bass_utils import run_bass_kernel_spmd as _run

    nc = _bacc.Bacc("TRN2", target_bir_lowering=False, num_devices=1)
    arrays, args = {}, []
    for name in _INS:
        a = _np.ascontiguousarray(inputs[name])
        arrays[f"in_{name}_dram"] = a
        args.append(nc.dram_tensor(f"in_{name}_dram", a.shape, _mybir.dt.from_np(a.dtype), kind="ExternalInput").ap())
    out = nc.dram_tensor("out_0_dram", (BATCH, N, D), F32, kind="ExternalOutput").ap()
    build(nc, *args, out)
    r = _run(nc, [arrays], core_ids=[0])
    return r.results[0]["out_0_dram"]
```

```python
from contextlib import ExitStack

import concourse.bass as bass
from concourse import mybir

F32 = mybir.dt.float32
BF16 = mybir.dt.bfloat16
I32 = mybir.dt.int32
ALU = mybir.AluOpType
ACT = mybir.ActivationFunctionType
AX = mybir.AxisListType

P = 128
BATCH, N, D = 4, 1024, 128
E, HID = 8, 512
HC = HID // P
TILES = BATCH * N // P
GROUPS = 2
GT = TILES // GROUPS
QUADS = GT // 4
ST = 256
SUB = ST // P
STILES = 2 * GT * P // ST + E
SROWS = STILES * ST
LOOPED = STILES // 4 - 2
assert 4 * LOOPED == GT
W2_AT = HID
B1_AT = W2_AT + HC * D
B2_AT = B1_AT + HC
WUSED = B2_AT + 1
WSTEP = B2_AT + 4
EPS_LN = 1e-5
XSLOTS = 4
YSLOTS = 2
GSLOTS = 8
BIG = 3e38
STORES = (GT, GT + 8, GT + 12, GT + 14, TILES)

HEADS = 16
DH = D // HEADS
SCALE = DH ** -0.5
EPS_RMS = 1.1920928955078125e-07
BT = N // P
PAIRS = HEADS // 2
SLOTS = 8
KROWS = SLOTS * DH
BLOCKS = 8
VW = 16
PSLOTS = 8
NB = BATCH * BLOCKS


MAX_BOUND = 60.0


class Plan:

    def __init__(self, blocks, bank, after=None):
        self.blocks = blocks
        keys = list(after.event) if after else []
        self.bank = dict(after.bank) if after else {}
        keys += [(kind, n) for block in blocks for kind, n, step in block if step is not None]
        self.event = {key: i for i, key in enumerate(keys)}
        for i, key in enumerate(keys):
            self.bank.setdefault(key, bank(i, *key))
        self.former = {}
        last = {}
        for i, key in enumerate(keys):
            self.former[key] = last.get(self.bank[key])
            last[self.bank[key]] = i


def weave(items, side, every):
    side, woven = list(side), []
    for i, item in enumerate(items):
        woven.append(item)
        if side and i % every == every - 1:
            woven += side.pop(0)
    return woven + [x for xs in side for x in xs]


def sums_of(g, i):
    return [("gather", g * GT + i + 3, None)] * (i + 3 < GT) + [("combine", g * GT + i, None)]


def turned(t):
    return [("turn_q", t, 0), ("turn_k", t, 0)]


def project(b):
    items = []
    for t in range(b * BT, (b + 1) * BT, 2):
        items += [("turn_x", t, 0), ("qkv", t, 0), ("qkv", t + 1, 0), ("sums", t, None), ("sums", t + 1, None)]
    return items + [("rsqrt", b, None)]


def first_batch():
    blocks = [[("gather", i, None) for i in range(3)]] + [sums_of(0, 2 * i) + sums_of(0, 2 * i + 1) for i in range(4)]
    blocks.append([("norm", 0, None)])
    blocks.append([("turn_x", 0, 0), ("qkv", 0, 1)])
    blocks.append([("qkv", 1, 0), ("turn_x", 2, 1), ("sums", 0, None), ("sums", 1, None)])
    blocks.append([("qkv", 2, 0), ("qkv", 3, 1)])
    blocks.append([("turn_x", 4, 0), ("sums", 2, None), ("sums", 3, None), ("qkv", 4, 1)])
    blocks.append([("qkv", 5, 0), ("turn_x", 6, 1), ("sums", 4, None), ("sums", 5, None)])
    blocks.append([("qkv", 6, 0), ("qkv", 7, 1), ("sums", 6, None), ("sums", 7, None)])
    blocks.append([("rsqrt", 0, None)])
    splits = [[("split", 0, None)]]
    for t in range(EARLY):
        more = [("split", t + 1, None)] * (t + 1 < EARLY)
        if t % 3 == 2:
            splits += [[("turn_q", t, 0), ("turn_k", t, 1)], more]
        else:
            splits.append([("turn_q", t, 0)] + more + [("turn_k", t, 1)])
    blocks += splits
    assert len(blocks) <= STILES
    for i in range(BT, GT):
        blocks[6 + i - BT] += sums_of(0, i)
    return blocks


def routing(ph, router=0):
    items = [("r_turn", ph * QUADS, 0)]
    for q in range(ph * QUADS, (ph + 1) * QUADS):
        items += [("r_turn", q + 1, 0)] * (q + 1 < (ph + 1) * QUADS) + [("router", q, 0)]
    return items + [("pick", ph, None), ("count", ph, 0), ("place", ph, None)]


def fast_plan():
    plan = [[]]
    sums = [sums_of(1, i) for i in range(GT)]
    for K in range(NB + 4):
        b, k = divmod(K, BLOCKS)
        before = [("turn_o", K - 1, 3)] if 1 <= K <= NB else []
        out = (lambda a, c: ([("turn_a", K - 4, a)], [("wo", K - 4, c)]) if K >= 4 else ([], []))
        items = [("evac_o", K - 1, None)] if 1 <= K <= NB else []
        if K == 0:
            for t in range(EARLY, BT):
                items += [("split", t, None), ("turn_q", t, t - EARLY + 1), ("turn_k", t, t - EARLY + 1)]
            items.append(("norm", 1, None))
            items += [("gather", GT + i, None) for i in range(3)]
        prep = K < NB and b + 1 < BATCH
        if prep and k < 4:
            t = BT * (b + 1) + 2 * k
            turn_a, wo = out(6, 7)
            items += before + [("turn_x", t, 4), ("qkv", t, 5), ("qkv", t + 1, 6)]
            items += turn_a + wo
            items += [("sums", t, None), ("sums", t + 1, None)]
            if k == 3:
                items.append(("rsqrt", b + 1, None))
        elif prep:
            t = BT * (b + 1) + 2 * (k - 4)
            turn_a, wo = out(4, 6)
            items += [("split", t, None)] + before + [("split", t + 1, None)] + turn_a
            items += [("turn_q", t, 5), ("turn_k", t, 5)] + wo + [("turn_q", t + 1, 7), ("turn_k", t + 1, 7)]
        else:
            turn_a, wo = out(5, 6)
            items += before + turn_a + wo
        if 1 <= K <= 5:
            n = 4 if K < 4 else 2
            items = weave(items, sums[:n], 2)
            sums = sums[n:]
        if k == 6 and b + 2 < BATCH:
            items.append(("norm", b + 2, None))
        r = GROUPS * QUADS
        if K == 24:
            items.append(("rnorm", 0, None))
        if K == 25:
            items.append(("rnorm", 1, None))
            items += [("r_turn", r, 7), ("r_turn", r + 1, 7)]
        if K == 26:
            items += [("router", r, 7), ("router", r + 1, 7), ("r_turn", r + 2, 7), ("r_turn", r + 3, 7)]
        if K == 27:
            items += [("router", r + 2, 7), ("router", r + 3, 7), ("pick", GROUPS, None)]
        if K == 28:
            items += [("count", GROUPS, 7), ("place", GROUPS, None)]
        if K == 29:
            items.append(("rnorm", 2, None))
        plan.append(items)
    assert not sums
    return plan


def general_plan():
    plan = []
    for b in range(BATCH):
        items = [("norm", b, None)] + project(b) if b else []
        for t in range(b * BT if b else EARLY, (b + 1) * BT):
            items += [("split", t, None)] + turned(t)
        if b == 0:
            items += [("gather", GT + i, None) for i in range(3)] + [x for i in range(GT) for x in sums_of(1, i)]
        items += [("general", b, None)]
        items += [x for t in range(b * BT, (b + 1) * BT) for x in (("turn_a", t, 0), ("wo", t, 0))]
        if b == 2:
            items += [("rnorm", n, None) for n in range(3)] + routing(GROUPS)
        plan.append(items)
    return plan


def routes():
    blocks = [routing(0), routing(1)]
    r = 3 * QUADS
    return blocks + [[("r_turn", r, 0)], [("router", r, 0), ("r_turn", r + 1, 0)],
                     [("router", r + 1, 0), ("r_turn", r + 2, 0)], [("router", r + 2, 0), ("r_turn", r + 3, 0)],
                     [("router", r + 3, 0)], [("pick", 3, None)], [("count", 3, 0)], [("place", 3, None)]]


EARLY = 8
PREFIX = Plan(first_batch(), lambda i, kind, n: 7)
FAST, GENERAL = (Plan(blocks, lambda i, kind, n: 6 + i % 2, PREFIX) for blocks in (fast_plan(), general_plan()))
ROUTES = Plan(routes(), lambda i, kind, n: 7 if i >= 2 * (2 * QUADS + 1) else i % 2)
BESIDE = ROUTES.blocks[2:]


class Link:

    def __init__(self, eng, sem, at=0):
        self.eng, self.sem, self.at = eng, sem, at

    def __call__(self, ins):
        ins.then_inc(self.sem, 1)
        self.at = self.at + 1
        self.eng.wait_ge(self.sem, self.at)


def build(nc, x_in, wq, wk, wv, wo, qn, kn, wr, br, w1, b1, w2, b2, out):
    xs_dram = [nc.dram_tensor(f"sorted_x{g}", [SROWS, D], F32).ap() for g in range(GROUPS)]
    ys_dram = [nc.dram_tensor(f"sorted_y{g}", [SROWS, D], F32).ap() for g in range(GROUPS)]

    with ExitStack() as ctx:
        def sb(name, shape, dt=F32):
            return ctx.enter_context(nc.sbuf_tensor(name, shape, dt))

        def sem(name):
            return ctx.enter_context(nc.semaphore(name))

        psum = ctx.enter_context(nc.psum_tensor("psum", [P, 8, 512], F32))
        bank = [psum[:, i, :] for i in range(8)]

        ident = sb("ident", [P, P])
        ones = sb("ones", [P, P])
        before = sb("before", [P, P])
        erow_i = sb("erow_i", [P, E], I32)
        erow = sb("erow", [P, E])
        trow_i = sb("trow_i", [P, STILES], I32)
        trow = sb("trow", [P, STILES])
        wr_sb = sb("wr_sb", [P, E])
        br_sb = sb("br_sb", [P, E])
        bias_rows = sb("bias_rows", [E * HC + E, P])
        weights = [sb(f"weights{f}", [P, E * WSTEP]) for f in range(2)]
        w_qkv = sb("w_qkv", [P, 3 * D])
        w_o = sb("w_o", [P, D])
        bias_cols = sb("bias_cols", [P, E * (HC + 1)])
        w_rows = sb("w_rows", [P, 4, D])
        w8 = sb("w8", [P, 3, DH])
        ident_b = sb("ident_b", [P, P], BF16)
        wview = [w[:, :].rearrange("p (e s) -> p e s", e=E) for w in weights]
        X = sb("X", [P, TILES, D])
        XN = sb("XN", [P, TILES, D])
        arena = sb("arena", [P, PSLOTS * 1024])
        at = [0]

        def carve(shape):
            n = 1
            for x in shape[1:]:
                n *= x
            view = arena[:, at[0]:at[0] + n]
            at[0] += n
            assert at[0] <= PSLOTS * 1024
            if len(shape) == 4:
                return view.rearrange("p (a b c) -> p a b c", a=shape[1], b=shape[2])
            return view.rearrange("p (a b) -> p a b", a=shape[1])

        probs = arena[:, :].rearrange("p (s n) -> p s n", s=PSLOTS)

        stats = sb("stats", [P, GT, 6])
        mv = sb("mv", [P, GT, 2])
        rin = sb("rin", [P, GT])
        rout = sb("rout", [P, GT])
        rtmp = sb("rtmp", [P, GT])
        xt = sb("xt", [P, 2, 512])
        sc = sb("sc", [P, GT, E])
        eq = sb("eq", [P, GT, E])
        oh = [sb(f"oh{k}", [P, GT, E]) for k in range(2)]
        both = sb("both", [P, GT, E])
        s2 = sb("s2", [P, GT, E])
        mx = [sb(f"mx{k}", [P, GT]) for k in range(2)]
        fst = sb("fst", [P, GT])
        diff = sb("diff", [P, GROUPS, GT])
        e2 = sb("e2", [P, GROUPS, GT])
        den = sb("den", [P, GT])
        gate = [sb(f"gate{k}", [P, TILES]) for k in range(2)]
        scan = [sb(f"scan{k}", [P, GT, E]) for k in range(2)]
        total = sb("total", [P, GT, E])
        within = sb("within", [P, GT, E])
        place = sb("place", [P, GT, E])
        cnt_i = sb("cnt_i", [P, 2, E], I32)
        cnt = sb("cnt", [P, 6, E])
        dst_f = sb("dst_f", [P, GT])
        dest = [sb(f"dest{k}", [P, TILES], I32) for k in range(2)]
        over = sb("over", [P, STILES, E])
        owner = sb("owner", [P, STILES])
        w_at = sb("w_at", [P, GROUPS, STILES], I32)

        xs = sb("xs", [P, XSLOTS, SUB, D])
        xst = carve([P, 2, ST])
        wbuf = carve([P, 2, WSTEP])
        hid = carve([P, 2, HC, ST])
        yt = carve([P, 2, ST])
        ys = sb("ys", [P, YSLOTS, SUB, D])
        gat = sb("gat", [P, GSLOTS, D])

        qk_at = [w[:, 0:2 * PAIRS * N // 2].bitcast(BF16).rearrange("p (s h n) -> p s h n", s=2, h=PAIRS)
                 for w in weights]
        qT = [qk_at[1][:, 0, :, :], qk_at[0][:, 0, :, :]]
        kT = [qk_at[1][:, 1, :, :], qk_at[0][:, 1, :, :]]
        zeros = weights[1][:, 0:2048]
        V = sb("V", [P, 2, BT, HEADS, VW])
        xa = sb("xa", [P, 2 * P])
        qk = sb("qk", [P, BT, 2 * D])
        sq = sb("sq", [P, 2, 2 * D])
        ss = sb("ss", [P, BT, 2 * HEADS])
        rs = sb("rs", [P, BT, 2 * HEADS])
        rst = sb("rst", [P, BT, 2 * HEADS])
        qh = sb("qh", [P, 2, 2 * D])
        rest = sb("rest", [P, 2 * D])
        stack = sb("stack", [P, 2, 2, HEADS, SLOTS, DH], BF16)
        oT = sb("oT", [P, 2, 512])
        osum = sb("osum", [P, 4, 4])
        att = xt[:, :, :].rearrange("p h (t d) -> p h t d", t=4)
        aT = sb("aT", [P, P])

        att8 = xt[:, :, :].rearrange("p h (t d) -> p (h t) d", t=4)
        reach = sb("reach", [P, 1])
        unbounded = sb("unbounded", [P, 1], I32)
        g_p, g_pt = arena[:, 0:1024], arena[:, 1024:2048]
        g_k = arena[:, 2048:2560].bitcast(BF16)
        g_q = arena[:, 2560:2624].bitcast(BF16)
        g_v = arena[:, 2624:2624 + BT * 2 * VW].rearrange("p (c r v) -> p c r v", c=BT, r=2)
        g_max = arena[:, 3000:3001]

        bounded = sem("bounded")
        attended = sem("attended")
        pool_alink = sem("pool_alink")
        dve_alink = sem("dve_alink")
        rs_ready = sem("rs_ready")
        normalised = sem("normalised")
        g_ready = sem("g_ready")
        g_scores = sem("g_scores")
        g_maxed = sem("g_maxed")
        g_exp = sem("g_exp")
        g_turned = sem("g_turned")
        g_copied = sem("g_copied")
        g_out = sem("g_out")
        g_done = sem("g_done")
        xnorm = sem("xnorm")
        scores_full = sem("scores_full")
        exp_done = sem("exp_done")
        pv_done = sem("pv_done")
        ot_full = sem("ot_full")
        aux_full = sem("aux_full")
        aux_read = sem("aux_read")
        squared = sem("squared")
        summed = sem("summed")
        
        stacked = sem("stacked")
        w_turned = sem("w_turned")
        w_copied = sem("w_copied")
        a_loaded = sem("a_loaded")
        w_again = sem("w_again")
        x_loaded = [sem(f"x_loaded{g}") for g in range(GROUPS)]
        r_loaded = sem("r_loaded")
        w_loaded = sem("w_loaded")
        b_loaded = sem("b_loaded")
        filled = [sem(f"filled{g}") for g in range(GROUPS)]
        consts = sem("consts")
        pool_link = sem("pool_link")
        dve_link = sem("dve_link")
        bias_t = sem("bias_t")
        bias_in = sem("bias_in")
        xn_ready = sem("xn_ready")
        diff_ready = sem("diff_ready")
        gate_exp = sem("gate_exp")
        r_full = sem("r_full")
        r_read = sem("r_read")
        picks = sem("picks")
        routed = sem("routed")
        scattered = [sem(f"scattered{g}") for g in range(GROUPS)]
        xs_in = [sem(f"xs_in{k}") for k in range(XSLOTS)]
        ys_out = [sem(f"ys_out{k}") for k in range(YSLOTS)]
        g_in = [sem(f"g_in{k}") for k in range(GSLOTS)]
        xs_turned = sem("xs_turned")
        xst_full = sem("xst_full")
        w_full = sem("w_full")
        h_full = sem("h_full")
        relu_done = sem("relu_done")
        y_full = sem("y_full")
        yt_full = sem("yt_full")
        o_full = sem("o_full")
        ys_full = sem("ys_full")
        half_in = sem("half_in")
        combined = sem("combined")
        out_done = sem("out_done")

        LOADS_W = 1 + E
        PEEL = (1, 1 + LOOPED, 3, 1)

        def full(pl):
            return r_full if pl is ROUTES else aux_full

        def read(pl):
            return r_read if pl is ROUTES else aux_read

        def turned_rows(ph, q):
            if ph == GROUPS:
                return xs[:, 2 * (q % 2):2 * (q % 2) + 2, :, :].rearrange("p s j d -> p (s j d)")
            return xt[:, q % 2, :]
        FILLS = SROWS // (P * 16)

        block = ctx.enter_context(nc.Block())

        def branch(eng, attend):
            eng.wait_ge(bounded, 1)
            far = eng.value_load(unbounded[0:1, 0:1], min_val=0, max_val=1)
            with eng.If(far > 0):
                attend(GENERAL)
            with eng.Else():
                attend(FAST)

        def sorted_quads(eng, step, peel=1):
            for t in range(4 * peel):
                step(t, t % 4, t == 0, False)
            if peel < 1 + LOOPED:
                with eng.Fori(peel, 1 + LOOPED) as q:
                    for j in range(4):
                        step(q * 4 + j, j, False, False)
            for j in range(4):
                step(STILES - 4 + j, j, False, j == 3)

        @block.sync
        def _(sp):
            xv = x_in.rearrange("b (n p) d -> p (b n) d", p=P)
            def load_x(g):
                sp.dma_start(X[:, g * GT:(g + 1) * GT, :], xv[:, g * GT:(g + 1) * GT, :]).then_inc(x_loaded[g], 16)

            def fill(g):
                for k in range(FILLS):
                    sp.dma_start(xs_dram[g][k * P * 16:(k + 1) * P * 16, :].rearrange("(n p) d -> p n d", p=P),
                                 zeros[:, :].rearrange("p (n d) -> p n d", d=D)).then_inc(filled[g], 16)

            def load_weights(f, sem):
                sp.dma_start(wview[f][:, :, 0:HID], w1.rearrange("e d h -> d e h")).then_inc(sem, 16)
                for e in range(E):
                    sp.dma_start(wview[f][:, e, W2_AT:B1_AT].rearrange("p (c d) -> p c d", c=HC),
                                 w2[e].rearrange("(c p) d -> p c d", p=P)).then_inc(sem, 16)

            load_x(0)
            sp.dma_start(wr_sb[:, :], wr).then_inc(r_loaded, 16)
            sp.dma_start(br_sb[:, :], br.rearrange("(a e) -> a e", a=1).to_broadcast([P, E])).then_inc(r_loaded, 16)
            sp.wait_ge(consts, 1)
            fill(0)
            load_x(1)
            sp.dma_start(bias_rows[0:E * HC, :], b1.rearrange("e (c p) -> (e c) p", p=P)).then_inc(b_loaded, 16)
            sp.dma_start(bias_rows[E * HC:, :], b2).then_inc(b_loaded, 16)
            for i, w in enumerate((wq, wk, wv, wo)):
                sp.dma_start(w_rows[:, i, :], w).then_inc(a_loaded, 16)
            for i, w in enumerate((qn, kn)):
                sp.dma_start(w8[:, i, :], w.rearrange("(a d) -> a d", a=1).to_broadcast([P, DH]))\
                    .then_inc(a_loaded, 16)
            load_weights(0, w_loaded)
            fill(1)

            def experts(f, g):
                ph = GROUPS * f + g
                base = ph * STILES
                if g == 0:
                    sp.wait_ge(scattered[g], 16 * 2 * GT * (f + 1))

                def load(t, slot, g=g):
                    sp.dma_start(xs[:, slot, :, :],
                                 xs_dram[g][bass.ds(t * ST, ST), :].rearrange("(j p) d -> p j d", p=P))\
                        .then_inc(xs_in[slot], 16)

                if g == 0:
                    for t in range(XSLOTS - 1):
                        if ph:
                            sp.wait_ge(xs_turned, base)
                        load(t, t)

                def step(t, slot, first, last):
                    if not isinstance(t, int) or t + XSLOTS - 1 < STILES:
                        if not (ph == 0 and first):
                            sp.wait_ge(xs_turned, t + base)
                        load(t + XSLOTS - 1, (slot + XSLOTS - 1) % XSLOTS)
                    elif g == 0:
                        n = t + XSLOTS - 1 - STILES
                        if n == 0:
                            sp.wait_ge(scattered[1], 16 * 2 * GT * (f + 1))
                        sp.wait_ge(xs_turned, t + base)
                        load(n, n, 1)
                    sp.wait_ge(ys_full, t + (base + 1))
                    sp.dma_start(ys_dram[g][bass.ds(t * ST, ST), :].rearrange("(j p) d -> p j d", p=P),
                                 ys[:, slot % YSLOTS, :, :]).then_inc(ys_out[slot % YSLOTS], 16)

                sorted_quads(sp, step)

            for g in range(GROUPS):
                experts(0, g)

            def reload(pl):
                if pl is FAST:
                    sp.wait_ge(pv_done, 8 * BLOCKS * (BATCH - 1))
                else:
                    sp.wait_ge(attended, 1)
                load_weights(1, w_again)

            branch(sp, reload)
            for g in range(GROUPS):
                experts(1, g)
            at = 0
            ov = out.rearrange("b (n p) d -> p (b n) d", p=P)
            for to in STORES:
                sp.wait_ge(combined, TILES + to)
                sp.dma_start(ov[:, at:to, :], X[:, at:to, :]).then_inc(out_done, 16)
                at = to
            sp.wait_ge(out_done, 16 * len(STORES))

        @block.gpsimd
        def _(pool):
            link = Link(pool, pool_link)
            pool.memset(zeros[:, :], 0.0).then_inc(consts, 1)
            link(pool.memset(ident[:, :], 0.0))
            pool.affine_select(out=ident[:, :], in_=ident[:, :], compare_op=ALU.not_equal, fill=1.0, base=0,
                               pattern=[[-1, P]], channel_multiplier=1).then_inc(consts, 1)
            link(pool.memset(before[:, :], 0.0))
            pool.affine_select(out=before[:, :], in_=before[:, :], compare_op=ALU.is_ge, fill=1.0, base=0,
                               pattern=[[-1, P]], channel_multiplier=1).then_inc(consts, 1)
            pool.iota(erow_i[:, :], pattern=[[-1, E]], base=E, channel_multiplier=0)
            link(pool.iota(trow_i[:, :], pattern=[[1, STILES]], base=0, channel_multiplier=0))
            pool.tensor_copy(erow[:, :], erow_i[:, :])
            pool.tensor_copy(trow[:, :], trow_i[:, :])
            pool.memset(ones[:, :], 1.0).then_inc(consts, 1)

            def scatter(f, g):
                ph = GROUPS * f + g
                if not f:
                    pool.wait_ge(filled[g], 16 * FILLS)
                pool.wait_ge(routed, ph + 1)
                for i in range(g * GT, (g + 1) * GT):
                    for k in range(2):
                        pool.indirect_dma_start(xs_dram[g], bass.IndirectOffsetOnAxis(ap=dest[k][:, i:i + 1], axis=0),
                                                XN[:, i, :], None).then_inc(scattered[g], 16)

            def gather(f, g, i):
                ph = GROUPS * f + g
                if i == 0:
                    for k in range(YSLOTS):
                        pool.wait_ge(ys_out[k], 16 * (STILES // YSLOTS) * (ph + 1))
                for k in range(2):
                    n = 2 * (ph * GT + i) + k
                    if n >= GSLOTS:
                        pool.wait_ge(combined, (n - GSLOTS) // 2 + 1)
                    pool.indirect_dma_start(gat[:, n % GSLOTS, :], None, ys_dram[g],
                                            bass.IndirectOffsetOnAxis(ap=dest[k][:, g * GT + i:g * GT + i + 1],
                                                                      axis=0)).then_inc(g_in[n % GSLOTS], 16)

            alink = Link(pool, pool_alink)

            def square(pl, t):
                pool.wait_ge(aux_read, pl.event["qkv", t] + 1)
                if t >= 2:
                    pool.wait_ge(summed, t - 1)
                pool.tensor_tensor(sq[:, t % 2, :], qk[:, t % BT, :], qk[:, t % BT, :], ALU.mult).then_inc(squared, 1)

            def normalise(t, alink):
                heads = qh[:, t % 2, :].rearrange("p (h d) -> p h d", d=DH)
                keys = heads[:, HEADS:, :]
                pool.wait_ge(rs_ready, t // BT + 1)
                if t >= 2:
                    pool.wait_ge(stacked, t - 1)
                alink(pool.tensor_tensor(heads, qk[:, t % BT, :].rearrange("p (h d) -> p h d", d=DH),
                                         rs[:, t % BT, :].unsqueeze(2).to_broadcast([P, 2 * HEADS, DH]), ALU.mult))
                pool.tensor_tensor(keys, keys, w8[:, 2, :].unsqueeze(1).to_broadcast([P, HEADS, DH]), ALU.mult)\
                    .then_inc(normalised, 1)

            def attend(pl, alink=alink):
                alink.at = 0 if alink is not link else link.at
                for items in pl.blocks:
                    for kind, n, _ in items:
                        if kind == "sums":
                            square(pl, n)
                        elif kind == "split":
                            normalise(n, alink)
                        elif kind == "gather":
                            gather(0, *divmod(n, GT))
                        elif kind == "place":
                            scatter(1, 0)

            for g in range(GROUPS):
                scatter(0, g)
            link(pool.memset(V[:, :, :, :, :], 0.0))
            pool.memset(V[:, :, :, :, DH:DH + 1], 1.0).then_inc(consts, 1)
            attend(PREFIX, link)
            branch(pool, attend)
            scatter(1, 1)
            for g in range(GROUPS):
                for i in range(GT):
                    gather(1, g, i)

        @block.vector
        def _(dve):
            link = Link(dve, dve_link)
            alink = Link(dve, dve_alink)

            def rsqrt(dst, src, tmp, link=link):
                link(dve.tensor_scalar(tmp.bitcast(I32), src.bitcast(I32), 1, None, ALU.logical_shift_right))
                link(dve.tensor_scalar(dst.bitcast(I32), tmp.bitcast(I32), -1.0, float(0x5f3759df), ALU.mult, ALU.add))
                for _ in range(3):
                    link(dve.tensor_tensor(tmp, dst, dst, ALU.mult))
                    link(dve.scalar_tensor_tensor(out=tmp, in0=tmp, scalar=-0.5, in1=src, op0=ALU.mult, op1=ALU.mult))
                    link(dve.scalar_tensor_tensor(out=dst, in0=tmp, scalar=1.5, in1=dst, op0=ALU.add, op1=ALU.mult))

            def layer_norm(tiles, ready, link=link):
                n = len(tiles)
                for i, t in enumerate(tiles):
                    last = dve.bn_stats(stats[:, i, :], X[:, t, :])
                link(last)
                for i in range(n):
                    last = dve.bn_aggr(mv[:, i, :], stats[:, i, :])
                link(last)
                link(dve.tensor_scalar(rin[:, 0:n], mv[:, 0:n, 1], EPS_LN, None, ALU.add))
                rsqrt(rout[:, 0:n], rin[:, 0:n], rtmp[:, 0:n], link)
                for i, t in enumerate(tiles):
                    dve.tensor_scalar(XN[:, t, :], X[:, t, :], mv[:, i, 0:1], rout[:, i:i + 1],
                                      ALU.subtract, ALU.mult).then_inc(ready, 1)

            def wide(ap):
                return ap.unsqueeze(2).to_broadcast([P, GT, E])

            def norm_routed(f, tiles, link):
                if f:
                    dve.wait_ge(scattered[tiles[0] // GT], 16 * 2 * GT)
                layer_norm(tiles, xn_ready, link)

            def pick(ph, link):
                for k, s in enumerate((sc, s2)):
                    link(dve.tensor_reduce(mx[k][:, :], s[:, :, :], AX.X, ALU.max))
                    link(dve.tensor_tensor(eq[:, :, :], s[:, :, :], wide(mx[k][:, :]), ALU.is_equal))
                    link(dve.tensor_tensor(eq[:, :, :], eq[:, :, :],
                                           erow[:, :].unsqueeze(1).to_broadcast([P, GT, E]), ALU.mult))
                    link(dve.tensor_reduce(fst[:, :], eq[:, :, :], AX.X, ALU.max))
                    link(dve.tensor_tensor(oh[k][:, :, :], eq[:, :, :], wide(fst[:, :]), ALU.is_equal))
                    if k == 0:
                        link(dve.scalar_tensor_tensor(out=s2[:, :, :], in0=oh[0][:, :, :], scalar=-BIG,
                                                      in1=sc[:, :, :], op0=ALU.mult, op1=ALU.add))
                dve.tensor_tensor(both[:, :, :], oh[0][:, :, :], oh[1][:, :, :], ALU.add).then_inc(picks, 1)
                dve.tensor_tensor(diff[:, ph % GROUPS, :], mx[1][:, :], mx[0][:, :], ALU.subtract)\
                    .then_inc(diff_ready, 1)

            def gates(f, g):
                ph = GROUPS * f + g
                cols = slice(g * GT, (g + 1) * GT)
                dve.wait_ge(gate_exp, ph + 1)
                link(dve.tensor_scalar(den[:, :], e2[:, g, :], 1.0, None, ALU.add))
                link(dve.reciprocal(den[:, :], den[:, :]))
                link(dve.tensor_scalar(gate[0][:, cols], den[:, :], 0.5, None, ALU.mult))
                link(dve.tensor_tensor(gate[1][:, cols], gate[0][:, cols], e2[:, g, :], ALU.mult))

            def place_rows(ph, link):
                g = ph % GROUPS
                cols = slice(g * GT, (g + 1) * GT)
                src, s, k = total, 1, 0
                while s < GT:
                    dve.tensor_copy(scan[k][:, 0:s, :], src[:, 0:s, :])
                    link(dve.tensor_tensor(scan[k][:, s:GT, :], src[:, s:GT, :], src[:, 0:GT - s, :], ALU.add))
                    src, s, k = scan[k], 2 * s, 1 - k
                dve.tensor_tensor(place[:, :, :], src[:, :, :], total[:, :, :], ALU.subtract)
                link(dve.tensor_scalar(cnt_i[:, 0, :], src[:, GT - 1, :], float(ST - 1), None, ALU.add))
                link(dve.tensor_scalar(cnt_i[:, 1, :], cnt_i[:, 0, :], ST.bit_length() - 1, None,
                                       ALU.logical_shift_right))
                link(dve.tensor_copy(cnt[:, 0, :], cnt_i[:, 1, :]))
                for n, s in enumerate((1, 2, 4)):
                    dve.tensor_copy(cnt[:, n + 1, 0:s], cnt[:, n, 0:s])
                    link(dve.tensor_tensor(cnt[:, n + 1, s:E], cnt[:, n, s:E], cnt[:, n, 0:E - s], ALU.add))
                link(dve.tensor_tensor(cnt[:, 4, :], cnt[:, 3, :], cnt[:, 0, :], ALU.subtract))
                link(dve.tensor_scalar(cnt[:, 5, :], cnt[:, 4, :], float(ST), None, ALU.mult))
                link(dve.tensor_tensor(place[:, :, :], place[:, :, :], within[:, :, :], ALU.add))
                link(dve.tensor_tensor(place[:, :, :], place[:, :, :],
                                       cnt[:, 5, :].unsqueeze(1).to_broadcast([P, GT, E]), ALU.add))
                for k in range(2):
                    link(dve.tensor_tensor(eq[:, :, :], oh[k][:, :, :], place[:, :, :], ALU.mult))
                    link(dve.tensor_reduce(dst_f[:, :], eq[:, :, :], AX.X, ALU.add))
                    link(dve.tensor_copy(dest[k][:, cols], dst_f[:, :]))
                link(dve.tensor_tensor(over[:, :, :], cnt[:, 3, :].unsqueeze(1).to_broadcast([P, STILES, E]),
                                       trow[:, :].unsqueeze(2).to_broadcast([P, STILES, E]), ALU.is_le))
                link(dve.tensor_reduce(owner[:, :], over[:, :, :], AX.X, ALU.add))
                dve.tensor_scalar(w_at[:, g, :], owner[:, :], float(E - 1), float(WSTEP), ALU.min, ALU.mult)\
                    .then_inc(routed, 1)

            def combine(f, g, i, j):
                ph = GROUPS * f + g
                x = X[:, bass.ds(i + g * GT, 1), :].rearrange("p a d -> p (a d)")
                for k in range(2):
                    dve.wait_ge(g_in[2 * j + k], (i - j) * 4 + 16 * (ph * QUADS + 1))
                    ins = dve.scalar_tensor_tensor(out=x, in0=gat[:, 2 * j + k, :],
                                                   scalar=gate[k][:, bass.ds(i + g * GT, 1)], in1=x,
                                                   op0=ALU.mult, op1=ALU.add)
                    if k == 0:
                        ins.then_inc(half_in, 1)
                        dve.wait_ge(half_in, i + (ph * GT + 1))
                    else:
                        ins.then_inc(combined, 1)

            def experts(f, g):
                ph = GROUPS * f + g
                base = ph * STILES
                beside = ph == GROUPS

                def turned(t, slot):
                    dve.wait_ge(xs_turned, t + (base + 1))
                    dve.tensor_copy(xst[:, slot % 2, :], bank[4][:, 0:ST]).then_inc(xst_full, 1)

                def rows(t, slot):
                    dve.wait_ge(o_full, t + (base + 1))
                    if not isinstance(t, int) or t >= YSLOTS:
                        dve.wait_ge(ys_out[slot % 2], (t - slot % 2) * 8 + 16 * (STILES // 2) * ph)
                    elif ph:
                        dve.wait_ge(ys_out[slot % 2], 16 * (STILES // 2) * ph)
                    dve.tensor_copy(ys[:, slot % 2, :, :], bank[5][:, 0:ST].rearrange("p (j d) -> p j d", d=D))\
                        .then_inc(ys_full, 1)

                turned(0, 0)

                def step(t, slot, first, last):
                    if not last:
                        turned(t + 1, slot + 1)
                    if not first:
                        rows(t - 1, slot - 1 + 4)
                    if ph == 3 and (not isinstance(t, int) or 4 <= t < 4 + GT):
                        combine(f, g - 1, t - 4, slot)
                    if ph == 1 and t < len(PREFIX.blocks):
                        aside(PREFIX, PREFIX.blocks[t], link)
                    if beside and first:
                        norm_routed(1, range(TILES - BT, TILES), link)
                    elif beside and isinstance(t, int) and t <= len(BESIDE):
                        aside(ROUTES, BESIDE[t - 1], link)

                sorted_quads(dve, step, PEEL[ph])
                rows(STILES - 1, 3)


            def place_biases(f):
                dve.tensor_copy(wview[f][:, :, B1_AT:B2_AT], bias_cols[:, 0:E * HC].rearrange("p (e c) -> p e c", e=E))
                dve.tensor_copy(wview[f][:, :, B2_AT], bias_cols[:, E * HC:]).then_inc(bias_in, 1)

            def evac_o(pl, K):
                dve.wait_ge(pv_done, 8 * (K + 1))
                if K >= 2:
                    dve.wait_ge(aux_full, pl.event["turn_o", K - 2] + 1)
                dve.tensor_copy(oT[:, K % 2, :], bank[4 + K % 2]).then_inc(ot_full, 1)

            def norm(b, link):
                dve.wait_ge(combined, (b + 1) * BT)
                layer_norm(range(b * BT, (b + 1) * BT), xnorm, link)

            def sums(t):
                dve.wait_ge(squared, t + 1)
                dve.tensor_reduce(ss[:, t % BT, :], sq[:, t % 2, :].rearrange("p (h d) -> p h d", d=DH),
                                  AX.X, ALU.add).then_inc(summed, 1)

            def rsqrt_qk(b, alink):
                dve.wait_ge(summed, (b + 1) * BT)
                alink(dve.tensor_scalar(ss[:, :, :], ss[:, :, :], 1.0 / DH, EPS_RMS, ALU.mult, ALU.add))
                rsqrt(*(a[:, :, :].rearrange("p t h -> p (t h)") for a in (rs, ss, rst)), alink)
                dve.sem_inc(rs_ready, 1)

            def split(pl, t, alink):
                u = t % 2
                dve.wait_ge(normalised, t + 1)
                if t >= 2:
                    dve.wait_ge(aux_full, pl.event["turn_k", t - 2] + 1)
                whole = qh[:, u, :].rearrange("p (a h d) -> p a h d", a=2, d=DH)
                left = rest[:, :].rearrange("p (a h d) -> p a h d", a=2, d=DH)
                first = [stack[:, u, a, :, 0, :] for a in range(2)]
                second = [stack[:, u, 0, :, 3, :], stack[:, u, 1, :, 1, :]]

                def wide(ap, n):
                    return ap.unsqueeze(2).to_broadcast([P, HEADS, n, DH])

                dve.tensor_copy(stack[:, u, 0, :, 0:3, :], wide(whole[:, 0], 3))
                alink(dve.tensor_copy(stack[:, u, 1, :, 0:SLOTS:3, :], wide(whole[:, 1], 3)))
                for a in range(2):
                    last = dve.tensor_tensor(left[:, a], whole[:, a], first[a], ALU.subtract)
                alink(last)
                dve.tensor_copy(stack[:, u, 0, :, 3:6, :], wide(left[:, 0], 3))
                alink(dve.tensor_copy(stack[:, u, 1, :, 1:SLOTS:3, :], wide(left[:, 1], 3)))
                dve.tensor_tensor(stack[:, u, 0, :, 6:8, :], wide(left[:, 0], 2), wide(second[0], 2), ALU.subtract)
                dve.tensor_tensor(stack[:, u, 1, :, 2:SLOTS:3, :], wide(left[:, 1], 2), wide(second[1], 2),
                                  ALU.subtract).then_inc(stacked, 1)

            def empty(pl, kind, n, link):
                src = bank[pl.bank[kind, n]]
                dve.wait_ge(full(pl), pl.event[kind, n] + 1)
                if kind == "turn_x":
                    ins = dve.tensor_copy(xa[:, :], src[:, 0:2 * P])
                elif kind == "qkv":
                    dve.tensor_copy(qk[:, n % BT, :], src[:, 0:2 * D])
                    ins = dve.tensor_copy(V[:, n // BT % 2, n % BT, :, 0:DH],
                                          src[:, 2 * D:3 * D].rearrange("p (h d) -> p h d", d=DH))
                elif kind in ("turn_q", "turn_k"):
                    to = (qT if kind == "turn_q" else kT)[n // BT % 2][:, :, n % BT * P:(n % BT + 1) * P]
                    ins = dve.tensor_scalar(to.bitcast(I32), src.bitcast(I32).rearrange("p (h n) -> p h n", h=PAIRS),
                                            0, None, ALU.logical_shift_right)
                elif kind == "turn_o":
                    half, g = divmod(n, 4)
                    v = src.rearrange("p (t j r) -> p t j r", t=4, j=4)
                    alink(dve.reciprocal(osum[:, :, :], v[:, :, :, DH]))
                    ins = dve.tensor_tensor(
                        att[:, half % 2, :, g * 4 * DH:(g + 1) * 4 * DH].rearrange("p t (j d) -> p t j d", d=DH),
                        v[:, :, :, 0:DH], osum[:, :, :].unsqueeze(3).to_broadcast([P, 4, 4, DH]), ALU.mult)
                elif kind == "turn_a":
                    ins = dve.tensor_copy(aT[:, :], src[:, 0:P])
                elif kind == "wo":
                    ins = dve.tensor_tensor(X[:, n, :], src[:, 0:D], X[:, n, :], ALU.add)
                elif kind == "r_turn":
                    ph, q = divmod(n, QUADS)
                    if q >= 2:
                        dve.wait_ge(full(pl), pl.event["router", n - 2] + 1)
                    ins = dve.tensor_copy(turned_rows(ph, q), src)
                elif kind == "router":
                    q = n % QUADS
                    ins = dve.tensor_tensor(sc[:, 4 * q:4 * q + 4, :],
                                            src[:, 0:4 * E].rearrange("p (t e) -> p t e", e=E),
                                            br_sb[:, :].unsqueeze(1).to_broadcast([P, 4, E]), ALU.add)
                    if q == QUADS - 1:
                        link(ins)
                        ins = None
                elif kind == "count":
                    dve.tensor_copy(within[:, :, :], src[:, 0:GT * E].rearrange("p (t e) -> p t e", e=E))
                    link(dve.tensor_copy(total[:, :, :],
                                         src[:, GT * E:2 * GT * E].rearrange("p (t e) -> p t e", e=E)))
                    ins = None
                if ins is None:
                    dve.sem_inc(read(pl), 1)
                else:
                    ins.then_inc(read(pl), 1)

            def general(pl, b):
                links, base = 5, alink.at
                dve.wait_ge(aux_read, pl.event["turn_k", (b + 1) * BT - 1] + 1)
                with dve.Fori(0, PAIRS) as pair:
                    with dve.Fori(0, BT) as i:
                        turn = pair * BT + i
                        at = (turn + b * PAIRS * BT) * 2
                        alink.at = turn * links + base
                        dve.tensor_copy(g_k, kT[b % 2][:, bass.ds(pair, 1), :].rearrange("p a n -> p (a n)"))
                        for r in range(2):
                            dve.tensor_copy(g_v[:, :, r, :],
                                            V[:, b % 2, :, bass.ds(pair * 2 + r, 1), :].rearrange("p c a v -> p c (a v)"))
                        alink(dve.tensor_copy(g_q, qT[b % 2][:, bass.ds(pair, 1), bass.ds(i * P, P)]
                                              .rearrange("p a n -> p (a n)")))
                        dve.sem_inc(g_ready, 1)
                        for r in range(2):
                            dve.wait_ge(g_scores, at + (r + 1))
                            dve.tensor_reduce(g_max, psum[:, 0:2, :].rearrange("p b n -> p (b n)"), AX.X, ALU.max,
                                              negate=True).then_inc(g_maxed, 1)
                            dve.wait_ge(g_turned, at + (r + 1))
                            dve.tensor_copy(g_pt, psum[:, 2:4, :].rearrange("p b n -> p (b n)")).then_inc(g_copied, 1)
                            dve.wait_ge(g_out, at + (r + 1))
                            alink(dve.reciprocal(osum[:, 0, 0:1], bank[4][:, DH:DH + 1]))
                            alink(dve.tensor_scalar(
                                att8[:, bass.ds(i, 1), bass.ds(pair * (2 * DH) + r * DH, DH)]
                                .rearrange("p a n -> p (a n)"),
                                bank[4][:, 0:DH], osum[:, 0, 0:1], None, ALU.mult))
                alink.at = base + PAIRS * BT * links
                dve.sem_inc(g_done, 1)

            def aside(pl, items, link):
                for kind, n, step in items:
                    if step is not None:
                        empty(pl, kind, n, link)
                    elif kind == "evac_o":
                        evac_o(pl, n)
                    elif kind == "norm":
                        norm(n, link)
                    elif kind == "sums":
                        sums(n)
                    elif kind == "rsqrt":
                        rsqrt_qk(n, link)
                    elif kind == "split":
                        split(pl, n, link)
                    elif kind == "general":
                        general(pl, n)
                    elif kind == "combine":
                        combine(0, *divmod(n, GT), n % 4)
                    elif kind == "rnorm":
                        norm_routed(1, range(n * BT, (n + 1) * BT), link)
                    elif kind == "pick":
                        pick(n, link)
                    elif kind == "place":
                        place_rows(n, link)

            def attend(pl):
                alink.at = 0
                dve.wait_ge(w_full, GROUPS * STILES)
                for items in pl.blocks:
                    aside(pl, items, alink)
                dve.wait_ge(aux_read, len(pl.event))
                dve.sem_inc(attended, 1)

            dve.memset(psum[:, 4:6, :], 0.0)
            dve.wait_ge(r_loaded, 16 * 2)
            for g in range(GROUPS):
                dve.wait_ge(x_loaded[g], 16)
                if g == 0:
                    dve.wait_ge(consts, 4)
                norm_routed(0, range(g * GT, (g + 1) * GT), link)
                aside(ROUTES, ROUTES.blocks[g], link)
            dve.tensor_copy(ident_b[:, :], ident[:, :])
            dve.wait_ge(a_loaded, 16 * 6)
            link(dve.tensor_tensor(w8[:, 2, :], w8[:, 0, :], w8[:, 1, :], ALU.mult))
            link(dve.tensor_scalar(w8[:, 2, :], w8[:, 2, :], SCALE, None, ALU.mult))
            link(dve.tensor_reduce(reach[:, :], w8[:, 2, :], AX.X, ALU.max, apply_absolute_value=True))
            dve.tensor_scalar(unbounded[:, :], reach[:, :], MAX_BOUND / DH, None, ALU.is_gt).then_inc(bounded, 1)
            dve.wait_ge(w_turned, 1)
            dve.tensor_copy(w_qkv[:, :], bank[6][:, 0:3 * D])
            dve.tensor_copy(w_o[:, :], bank[6][:, 3 * D:4 * D]).then_inc(w_copied, 1)
            dve.wait_ge(bias_t, 1)
            link(dve.tensor_copy(bias_cols[:, :], bank[7][:, 0:E * (HC + 1)]))
            place_biases(0)
            experts(0, 0)
            gates(0, 0)
            dve.wait_ge(consts, 5)
            experts(0, 1)
            gates(0, 1)
            branch(dve, attend)
            dve.wait_ge(w_again, 16 * (1 + E))
            place_biases(1)
            experts(1, 0)
            gates(1, 0)
            experts(1, 1)
            gates(1, 1)
            for i in range(GT):
                combine(1, 1, i, i % 4)

        @block.scalar
        def _(act):
            def gate(f, g):
                act.wait_ge(diff_ready, GROUPS * f + g + 1)
                act.activation(e2[:, g, :], diff[:, g, :], ACT.Exp).then_inc(gate_exp, 1)

            def experts(f, g):
                ph = GROUPS * f + g
                base = ph * STILES

                def fetch(t, slot):
                    at = act.value_load(w_at[0:1, g, bass.ds(t, 1)], min_val=0, max_val=(E - 1) * WSTEP)
                    if not (ph == 0 and isinstance(t, int) and t < 2):
                        act.wait_ge(yt_full, t + (base - 1))
                    act.activation(wbuf[:, slot % 2, 0:WUSED], weights[f][:, bass.ds(at, WUSED)], ACT.Copy)\
                        .then_inc(w_full, 1)

                act.wait_ge(routed, ph + 1)
                fetch(0, 0)

                def step(t, slot, first, last):
                    for c in range(HC):
                        act.wait_ge(h_full, t * HC + (base * HC + c + 1))
                        act.activation(hid[:, slot % 2, c, :], bank[c][:, 0:ST], ACT.Relu,
                                       bias=wbuf[:, slot % 2, B1_AT + c:B1_AT + c + 1]).then_inc(relu_done, 1)
                    if not last:
                        fetch(t + 1, slot + 1)
                    act.wait_ge(y_full, t + (base + 1))
                    act.activation(yt[:, slot % 2, :], bank[6][:, 0:ST], ACT.Identity,
                                   bias=wbuf[:, slot % 2, B2_AT:B2_AT + 1]).then_inc(yt_full, 1)

                sorted_quads(act, step)

            def attend(pl):
                if pl is GENERAL:
                    with act.Fori(0, NB * 2 * BT) as n:
                        act.wait_ge(g_maxed, n + 1)
                        act.activation(g_p, psum[:, 0:2, :].rearrange("p b n -> p (b n)"), ACT.Exp,
                                       bias=g_max).then_inc(g_exp, 1)
                    return

                def block(K):
                    for u in range(16):
                        act.wait_ge(scores_full, K * 16 + (u + 1))
                        if u >= PSLOTS or not isinstance(K, int):
                            act.wait_ge(pv_done, K * 8 + (u // 2 + 1 - PSLOTS // 2))
                        act.activation(probs[:, u % PSLOTS, :],
                                       psum[:, 2 * (u % 2):2 * (u % 2) + 2, :].rearrange("p b n -> p (b n)"),
                                       ACT.Exp).then_inc(exp_done, 1)

                block(0)
                with act.Fori(1, NB) as K:
                    block(K)

            for g in range(GROUPS):
                gate(0, g)
            act.wait_ge(w_loaded, 16 * LOADS_W)
            act.wait_ge(bias_in, 1)
            for g in range(GROUPS):
                experts(0, g)
            branch(act, attend)
            act.wait_ge(bias_in, 2)
            for g in range(GROUPS):
                gate(1, g)
                experts(1, g)

        @block.tensor
        def _(pe):
            def experts(f, g):
                ph = GROUPS * f + g
                base = ph * STILES

                def turn(t, slot, first=False):
                    pe.wait_ge(xs_in[slot % XSLOTS], (t - slot % XSLOTS) * 4 + 16 * (STILES // 4 * ph + 1))
                    if not (ph == 0 and first):
                        pe.wait_ge(xst_full, t + base)
                    for j in range(SUB):
                        mm = pe.transpose(bank[4][:, j * P:(j + 1) * P], xs[:, slot % XSLOTS, j, :], ident[:, :])
                    mm.then_inc(xs_turned, 1)

                def back(t, slot, first=False):
                    pe.wait_ge(yt_full, t + (base + 1))
                    if not (ph == 0 and first):
                        pe.wait_ge(ys_full, t + base)
                    for j in range(SUB):
                        mm = pe.transpose(bank[5][:, j * P:(j + 1) * P], yt[:, slot % 2, j * P:(j + 1) * P],
                                          ident[:, :])
                    mm.then_inc(o_full, 1)

                turn(0, 0, True)

                def step(t, slot, first, last):
                    if not last:
                        turn(t + 1, slot + 1)
                    pe.wait_ge(xst_full, t + (base + 1))
                    pe.wait_ge(w_full, t + (base + 1))
                    for c in range(HC):
                        pe.matmul(bank[c][:, 0:ST], wbuf[:, slot % 2, c * P:(c + 1) * P], xst[:, slot % 2, :],
                                  start=True, stop=True).then_inc(h_full, 1)
                    if not first:
                        back(t - 1, slot - 1 + 4, isinstance(t, int) and t == 1)
                    if ph == GROUPS and isinstance(t, int) and 1 <= t <= len(BESIDE):
                        if t == 1:
                            pe.wait_ge(attended, 1)
                        fills(ROUTES, BESIDE[t - 1])
                    if ph == 1 and t < len(PREFIX.blocks):
                        fills(PREFIX, PREFIX.blocks[t], 0)
                    for c in range(HC):
                        pe.wait_ge(relu_done, t * HC + (base * HC + c + 1))
                        mm = pe.matmul(bank[6][:, 0:ST], wbuf[:, slot % 2, W2_AT + c * D:W2_AT + (c + 1) * D],
                                       hid[:, slot % 2, c, :], start=(c == 0), stop=(c == HC - 1))
                    mm.then_inc(y_full, 1)
                    if ph == 1 and t < len(PREFIX.blocks):
                        fills(PREFIX, PREFIX.blocks[t], 1)

                sorted_quads(pe, step, PEEL[ph])
                back(STILES - 1, 3)

            def fill(pl, kind, n):
                former = pl.former[kind, n]
                dst = bank[pl.bank[kind, n]]
                if former is not None:
                    pe.wait_ge(read(pl), former + 1)
                if kind == "turn_x":
                    for j in range(2):
                        pe.wait_ge(xnorm, n + j + 1)
                        mm = pe.transpose(dst[:, j * P:(j + 1) * P], XN[:, n + j, :], ident[:, :])
                elif kind == "qkv":
                    pe.wait_ge(aux_read, pl.event["turn_x", n - n % 2] + 1)
                    mm = pe.matmul(dst[:, 0:3 * D], xa[:, n % 2 * P:(n % 2 + 1) * P], w_qkv[:, :],
                                   start=True, stop=True)
                elif kind in ("turn_q", "turn_k"):
                    pe.wait_ge(stacked, n + 1)
                    flat = stack[:, n % 2, int(kind == "turn_k"), :, :, :].rearrange("p h s d -> p (h s d)")
                    for j in range(PAIRS):
                        mm = pe.transpose(dst.bitcast(BF16)[:, j * P:(j + 1) * P], flat[:, j * P:(j + 1) * P],
                                          ident_b[:, :])
                elif kind == "turn_o":
                    pe.wait_ge(ot_full, n + 1)
                    for j in range(4):
                        mm = pe.transpose(dst[:, j * P:(j + 1) * P], oT[:, n % 2, j * P:(j + 1) * P], ident[:, :])
                elif kind == "turn_a":
                    if pl is FAST:
                        pe.wait_ge(aux_read, pl.event["turn_o", n - n % 4 + 3] + 1)
                    else:
                        pe.wait_ge(g_done, n // BT + 1)
                    mm = pe.transpose(dst[:, 0:P], att8[:, n % 8, :], ident[:, :])
                elif kind == "wo":
                    pe.wait_ge(aux_read, pl.event["turn_a", n] + 1)
                    mm = pe.matmul(dst[:, 0:D], aT[:, :], w_o[:, :], start=True, stop=True)
                elif kind == "r_turn":
                    for j in range(4):
                        pe.wait_ge(xn_ready, 4 * n + j + 1)
                        mm = pe.transpose(dst[:, j * P:(j + 1) * P], XN[:, (4 * n + j) % TILES, :], ident[:, :])
                elif kind == "router":
                    pe.wait_ge(read(pl), pl.event["r_turn", n] + 1)
                    rows = turned_rows(*divmod(n, QUADS))
                    for j in range(4):
                        mm = pe.matmul(dst[:, j * E:(j + 1) * E], rows[:, j * P:(j + 1) * P], wr_sb[:, :],
                                       start=True, stop=True)
                elif kind == "count":
                    pe.wait_ge(picks, n + 1)
                    flat = both[:, :, :].rearrange("p t e -> p (t e)")
                    pe.matmul(dst[:, 0:GT * E], before[:, :], flat, start=True, stop=True)
                    mm = pe.matmul(dst[:, GT * E:2 * GT * E], ones[:, :], flat, start=True, stop=True)
                mm.then_inc(full(pl), 1)

            def scores(K, c, a):
                b, k = divmod(K, BLOCKS)
                half, g = divmod(k, 4)
                u = 16 * K + 2 * c + a
                pair = 2 * g + a
                if u >= 2:
                    pe.wait_ge(exp_done, u - 1)
                for r in range(2):
                    rows = slice(r * KROWS, (r + 1) * KROWS)
                    mm = pe.matmul(bank[2 * a + r], kT[b % 2][rows, pair, c * P:(c + 1) * P],
                                   qT[b % 2][rows, pair, half * 512:(half + 1) * 512], start=True, stop=True)
                mm.then_inc(scores_full, 1)

            def values(K, c):
                b, k = divmod(K, BLOCKS)
                g = k % 4
                if c == 0 and K >= 2:
                    pe.wait_ge(ot_full, K - 1)
                pe.wait_ge(exp_done, 16 * K + 2 * c + 2)
                for j in range(4):
                    u = 2 * c + j // 2
                    mm = pe.matmul(bank[4 + K % 2][32 * j:32 * j + VW, :], V[:, b % 2, c, 4 * g + j, :],
                                   probs[:, u % PSLOTS, j % 2 * 512:(j % 2 + 1) * 512],
                                   start=(c == 0), stop=(c == BT - 1))
                mm.then_inc(pv_done, 1)

            def fills(pl, block, at=None):
                for kind, n, step in block:
                    if step is not None and (at is None or step == at):
                        fill(pl, kind, n)

            def general(b):
                with pe.Fori(0, PAIRS * BT) as i:
                    turn = i + b * PAIRS * BT
                    pe.wait_ge(g_ready, turn + 1)
                    for r in range(2):
                        n = turn * 2 + (r + 1)
                        rows = slice(r * KROWS, (r + 1) * KROWS)
                        for h in range(2):
                            mm = pe.matmul(bank[h], g_q[rows, :], g_k[rows, h * 512:(h + 1) * 512],
                                           start=True, stop=True)
                        mm.then_inc(g_scores, 1)
                        pe.wait_ge(g_exp, n)
                        for c in range(BT):
                            mm = pe.transpose(bank[2 + c // 4][:, c % 4 * P:(c % 4 + 1) * P],
                                              g_p[:, c * P:(c + 1) * P], ident[:, :])
                        mm.then_inc(g_turned, 1)
                        pe.wait_ge(g_copied, n)
                        for c in range(BT):
                            mm = pe.matmul(bank[4][:, 0:VW], g_pt[:, c * P:(c + 1) * P], g_v[:, c, r, :],
                                           start=(c == 0), stop=(c == BT - 1))
                        mm.then_inc(g_out, 1)

            def attend(pl):
                if pl is GENERAL:
                    for items in pl.blocks:
                        for kind, n, step in items:
                            if kind == "general":
                                general(n)
                            elif step is not None:
                                fill(pl, kind, n)
                    return
                fills(pl, pl.blocks[0])
                LAG = 2
                for K in range(NB):
                    k = K % BLOCKS
                    if k == 0 and K:
                        pe.wait_ge(aux_read, pl.event["turn_k", (K // BLOCKS + 1) * BT - 1] + 1)
                    for c in range(BT):
                        if K == 0:
                            pe.wait_ge(aux_read, pl.event["turn_k", max(c, EARLY - 1)] + 1)
                        scores(K, c, 0)
                        s = 8 * k + c - LAG
                        if s >= 0:
                            values(K - k + s // 8, s % 8)
                        scores(K, c, 1)
                        fills(pl, pl.blocks[K + 1], c)
                    if k == BLOCKS - 1:
                        for c in range(BT - LAG, BT):
                            values(K, c)
                for K in range(NB, NB + 4):
                    fills(pl, pl.blocks[K + 1])

            pe.wait_ge(consts, 4)
            pe.wait_ge(r_loaded, 16 * 2)
            for g in range(GROUPS):
                fills(ROUTES, ROUTES.blocks[g])
            pe.wait_ge(a_loaded, 16 * 6)
            for i in range(4):
                mm = pe.transpose(bank[6][:, i * D:(i + 1) * D], w_rows[:, i, :], ident[:, :])
            mm.then_inc(w_turned, 1)
            pe.wait_ge(b_loaded, 32)
            pe.transpose(bank[7][:, 0:E * HC + E], bias_rows[:, :], ident[0:E * HC + E, 0:E * HC + E])\
                .then_inc(bias_t, 1)
            pe.wait_ge(w_copied, 1)
            pe.wait_ge(routed, 2)
            for g in range(GROUPS):
                experts(0, g)
            branch(pe, attend)
            for g in range(GROUPS):
                experts(1, g)


_INS = ['L0_attn_x', 'L0_attn_Wq', 'L0_attn_Wk', 'L0_attn_Wv', 'L0_attn_Wo', 'L0_attn_qn_w', 'L0_attn_kn_w',
        'L0_ffn_Wr', 'L0_ffn_br', 'L0_ffn_W1', 'L0_ffn_b1', 'L0_ffn_W2', 'L0_ffn_b2']


def kernel(**inputs):
    import numpy as _np
    import concourse.bacc as _bacc
    from concourse import mybir as _mybir
    from concourse.bass_utils import run_bass_kernel_spmd as _run

    nc = _bacc.Bacc("TRN2", target_bir_lowering=False, num_devices=1)
    arrays, args = {}, []
    for name in _INS:
        a = _np.ascontiguousarray(inputs[name])
        arrays[f"in_{name}_dram"] = a
        args.append(nc.dram_tensor(f"in_{name}_dram", a.shape, _mybir.dt.from_np(a.dtype), kind="ExternalInput").ap())
    out = nc.dram_tensor("out_0_dram", (BATCH, N, D), F32, kind="ExternalOutput").ap()
    build(nc, *args, out)
    r = _run(nc, [arrays], core_ids=[0])
    return r.results[0]["out_0_dram"]
```

```python
from contextlib import ExitStack

import concourse.bass as bass
from concourse import mybir

F32 = mybir.dt.float32
BF16 = mybir.dt.bfloat16
I32 = mybir.dt.int32
ALU = mybir.AluOpType
ACT = mybir.ActivationFunctionType
AX = mybir.AxisListType

P = 128
BATCH, N, D = 4, 1024, 128
E, HID = 8, 512
HC = HID // P
TILES = BATCH * N // P
SIZES = ((12, 20), (20, 12))
GROUPS = 2
GT = max(max(sizes) for sizes in SIZES)
ST = 256
SUB = ST // P
W2_AT = HID
B1_AT = W2_AT + HC * D
B2_AT = B1_AT + HC
WUSED = B2_AT + 1
WSTEP = B2_AT + 4
FILL = 4 * ST
EPS_LN = 1e-5
XSLOTS = 4
YSLOTS = 2
GSLOTS = 8
BIG = 3e38


class Group:

    def __init__(self, f, g, former):
        self.f, self.g, self.ph = f, g, GROUPS * f + g
        self.tiles = SIZES[f][g]
        self.start = sum(SIZES[f][:g])
        self.stiles = 2 * self.tiles * P // ST + E
        assert self.tiles % 4 == 0 and self.stiles % 4 == 0
        self.base = former.base + former.stiles if former else 0
        self.quads = range((f * TILES + self.start) // 4, (f * TILES + self.start + self.tiles) // 4)
        self.cols = slice(self.start, self.start + self.tiles)
        self.scattered = 16 * 2 * sum(SIZES[i][g] for i in range(f + 1))


PHASES = []
for _f in range(2):
    for _g in range(GROUPS):
        PHASES.append(Group(_f, _g, PHASES[-1] if PHASES else None))
FIRST = PHASES[:GROUPS]
SECOND = PHASES[GROUPS:]
STILES = max(G.stiles for G in PHASES)
SROWS = [max(G.stiles for G in PHASES if G.g == g) * ST for g in range(GROUPS)]
STORES = (20, 26, 29, 31, 32)

HEADS = 16
DH = D // HEADS
SCALE = DH ** -0.5
EPS_RMS = 1.1920928955078125e-07
BT = N // P
PAIRS = HEADS // 2
SLOTS = 8
KROWS = SLOTS * DH
BLOCKS = 8
VW = 16
PSLOTS = 8
NB = BATCH * BLOCKS


MAX_BOUND = 60.0


class Plan:

    def __init__(self, blocks, bank, after=None):
        self.blocks = blocks
        keys = list(after.event) if after else []
        self.bank = dict(after.bank) if after else {}
        keys += [(kind, n) for block in blocks for kind, n, step in block if step is not None]
        self.event = {key: i for i, key in enumerate(keys)}
        for i, key in enumerate(keys):
            self.bank.setdefault(key, bank(i, *key))
        self.former = {}
        last = {}
        for i, key in enumerate(keys):
            self.former[key] = last.get(self.bank[key])
            last[self.bank[key]] = i


def weave(items, side, every):
    side, woven = list(side), []
    for i, item in enumerate(items):
        woven.append(item)
        if side and i % every == every - 1:
            woven += side.pop(0)
    return woven + [x for xs in side for x in xs]


def sums_of(G, i):
    return [("gather", G.start + i + 3, None)] * (i + 3 < G.tiles) + [("combine", G.start + i, None)]


def turned(t):
    return [("turn_q", t, 0), ("turn_k", t, 0)]


def project(b):
    items = []
    for t in range(b * BT, (b + 1) * BT, 2):
        items += [("turn_x", t, 0), ("qkv", t, 0), ("qkv", t + 1, 0), ("sums", t, None), ("sums", t + 1, None)]
    return items + [("rsqrt", b, None)]


def first_batch():
    blocks = [[("gather", i, None) for i in range(3)]]
    blocks += [sums_of(FIRST[0], 2 * i) + sums_of(FIRST[0], 2 * i + 1) for i in range(BT // 2)]
    blocks.append([("norm", 0, None)])
    blocks.append([("turn_x", 0, 0), ("qkv", 0, 1)])
    blocks.append([("qkv", 1, 0), ("turn_x", 2, 1), ("sums", 0, None), ("sums", 1, None)])
    blocks.append([("qkv", 2, 0), ("qkv", 3, 1)])
    blocks.append([("turn_x", 4, 0), ("sums", 2, None), ("sums", 3, None), ("qkv", 4, 1)])
    blocks.append([("qkv", 5, 0), ("turn_x", 6, 1), ("sums", 4, None), ("sums", 5, None)])
    blocks.append([("qkv", 6, 0), ("qkv", 7, 1), ("sums", 6, None), ("sums", 7, None)])
    blocks.append([("rsqrt", 0, None)])
    splits = [[("split", 0, None)]]
    for t in range(EARLY):
        more = [("split", t + 1, None)] * (t + 1 < EARLY)
        if t % 3 == 2:
            splits += [[("turn_q", t, 0), ("turn_k", t, 1)], more]
        else:
            splits.append([("turn_q", t, 0)] + more + [("turn_k", t, 1)])
    blocks += splits
    for i in range(BT, FIRST[0].tiles):
        blocks[6 + i - BT] += sums_of(FIRST[0], i)
    assert len(blocks) <= FIRST[1].stiles
    return blocks


def routing(ph):
    quads = PHASES[ph].quads
    items = [("r_turn", quads[0], 0)]
    for q in quads:
        items += [("r_turn", q + 1, 0)] * (q + 1 in quads) + [("router", q, 0)]
    return items + [("pick", ph, None), ("count", ph, 0), ("place", ph, None)]


def fast_plan():
    plan = [[]]
    sums = [sums_of(FIRST[1], i) for i in range(FIRST[1].tiles)]
    for K in range(NB + 4):
        b, k = divmod(K, BLOCKS)
        before = [("turn_o", K - 1, 3)] if 1 <= K <= NB else []
        out = (lambda a, c: ([("turn_a", K - 4, a)], [("wo", K - 4, c)]) if K >= 4 else ([], []))
        items = [("evac_o", K - 1, None)] if 1 <= K <= NB else []
        if K == 0:
            for t in range(EARLY, BT):
                items += [("split", t, None), ("turn_q", t, t - EARLY + 1), ("turn_k", t, t - EARLY + 1)]
            items += [("gather", FIRST[1].start + i, None) for i in range(3)]
        prep = K < NB and b + 1 < BATCH
        first, last = BT * (b + 1), BT * (b + 2)
        if K in (1, 2):
            t = first + 4 * (K - 1)
            items += before + [("turn_x", t, 3), ("qkv", t, 4), ("qkv", t + 1, 5), ("turn_x", t + 2, 5),
                               ("sums", t, None), ("sums", t + 1, None), ("qkv", t + 2, 6), ("qkv", t + 3, 7),
                               ("sums", t + 2, None), ("sums", t + 3, None)]
            if K == 2:
                items.append(("rsqrt", 1, None))
        elif K == 0:
            items += before
        elif prep and k < 4 and b:
            t = first + 2 * k
            turn_a, wo = out(6, 7)
            items += before + [("turn_x", t, 4), ("qkv", t, 5), ("qkv", t + 1, 6)]
            items += turn_a + wo
            items += [("sums", t, None), ("sums", t + 1, None)]
            if k == 3:
                items.append(("rsqrt", b + 1, None))
        elif K == 3:
            t = first
            items += [("split", t, None)] + before + [("turn_q", t, 5), ("turn_k", t, 5)]
        elif K == 4:
            t = first + 1
            turn_a, wo = out(4, 6)
            items += [("split", t, None)] + before + turn_a + [("turn_q", t, 5), ("turn_k", t, 5)] + wo
        elif prep:
            ahead = [first + 2 * (k - 4), first + 2 * (k - 4) + 1]
            turn_a, wo = out(4, 6)
            t = ahead[0]
            items += [("split", t, None)] + before + [("split", t + 1, None)] + turn_a
            turns = [("turn_q", t, 5), ("turn_k", t, 5)]
            if k < BLOCKS - 1:
                items += turns + wo + [("turn_q", t + 1, 7), ("turn_k", t + 1, 7)]
            else:
                items += turns + [("turn_q", t + 1, 6), ("turn_k", t + 1, 6)] + out(4, 7)[1]
        else:
            turn_a, wo = out(5, 6)
            items += before + turn_a + wo
        if K == 0:
            n = 2 * BT - FIRST[1].start
            items = items + [x for i in range(n) for x in sums[i]] + [("norm", 1, None)]
            sums = sums[n:]
        elif sums:
            n = 3 if K < 5 else 2
            items = weave(items, sums[:n], 2)
            sums = sums[n:]
        if k == 6 and b + 2 < BATCH:
            items.append(("norm", b + 2, None))
        r = SECOND[0].quads[0]
        if K == 24:
            items = items[:1] + [("rnorm", 0, None)] + items[1:] + [("rnorm", 1, None)]
        if K == 25:
            items = items[:1] + [("rnorm", 2, None)] + items[1:] + [("r_turn", r, 7), ("r_turn", r + 1, 7)]
        if K == 26:
            items += [("router", r, 6), ("r_turn", r + 2, 6), ("router", r + 1, 7), ("r_turn", r + 3, 7)]
        if K == 27:
            items += [("router", r + 2, 6), ("r_turn", r + 4, 6), ("router", r + 3, 7)]
        if K == 28:
            items = [("router", r + 4, 0), ("pick", SECOND[0].ph, None)] + items
            items += [("count", SECOND[0].ph, 7), ("place", SECOND[0].ph, None)]
        if K == 29:
            items.append(("rnorm", 3, None))
        if K >= NB:
            n = K - 4
            items = items[:-2] + [("turn_a", n, 0)] * (K == NB) + [("turn_a", n + 1, 0)] * (n + 1 < NB) + [("wo", n, 0)]
            if K == NB:
                items = [(kind, m, None if step is None else 0) for kind, m, step in items]
        steps = [step for _, _, step in items if step is not None]
        assert steps == sorted(steps)
        plan.append(items)
    assert not sums
    return plan


def general_plan():
    plan = []
    for b in range(BATCH):
        items = [("norm", b, None)] + project(b) if b else []
        for t in range(b * BT if b else EARLY, (b + 1) * BT):
            items += [("split", t, None)] + turned(t)
        if b == 0:
            items += [("gather", FIRST[1].start + i, None) for i in range(3)]
            items += [x for i in range(FIRST[1].tiles) for x in sums_of(FIRST[1], i)]
        items += [("general", b, None)]
        items += [x for t in range(b * BT, (b + 1) * BT) for x in (("turn_a", t, 0), ("wo", t, 0))]
        if b == 2:
            items += [("rnorm", n, None) for n in range(4)] + routing(SECOND[0].ph)
        plan.append(items)
    return plan


def routes():
    blocks = [routing(0), routing(1)[:-3]]
    r = SECOND[1].quads[0]
    beside = {0: [[("pick", 1, None)], [("count", 1, 0)], [("place", 1, None)]],
              2: [[], [("r_turn", r, 0)], [("router", r, 0), ("r_turn", r + 1, 0)],
                  [("router", r + 1, 0), ("r_turn", r + 2, 0)], [("router", r + 2, 0)],
                  [("pick", 3, None)], [("count", 3, 0)], [("place", 3, None)]]}
    return blocks + beside[0] + beside[2], beside


NORMS = (range(0, 8), range(8, 16), range(16, 20), range(20, 24), range(24, 32))
EARLY = 8
PREFIX = Plan(first_batch(), lambda i, kind, n: 7)
FAST, GENERAL = (Plan(blocks, lambda i, kind, n: 6 + i % 2, PREFIX) for blocks in (fast_plan(), general_plan()))
_blocks, BESIDE = routes()
ROUTES = Plan(_blocks, lambda i, kind, n: 7 if i > 2 * TILES // 4 else i % 2)


class Link:

    def __init__(self, eng, sem, at=0):
        self.eng, self.sem, self.at = eng, sem, at

    def __call__(self, ins):
        ins.then_inc(self.sem, 1)
        self.at = self.at + 1
        self.eng.wait_ge(self.sem, self.at)


def build(nc, x_in, wq, wk, wv, wo, qn, kn, wr, br, w1, b1, w2, b2, out):
    xs_dram = [nc.dram_tensor(f"sorted_x{g}", [SROWS[g], D], F32).ap() for g in range(GROUPS)]
    ys_dram = [nc.dram_tensor(f"sorted_y{g}", [SROWS[g], D], F32).ap() for g in range(GROUPS)]

    with ExitStack() as ctx:
        def sb(name, shape, dt=F32):
            return ctx.enter_context(nc.sbuf_tensor(name, shape, dt))

        def sem(name):
            return ctx.enter_context(nc.semaphore(name))

        psum = ctx.enter_context(nc.psum_tensor("psum", [P, 8, 512], F32))
        bank = [psum[:, i, :] for i in range(8)]

        ident = sb("ident", [P, P])
        ones = sb("ones", [P, P])
        before = sb("before", [P, P])
        erow_i = sb("erow_i", [P, E], I32)
        erow = sb("erow", [P, E])
        trow_i = sb("trow_i", [P, STILES], I32)
        trow = sb("trow", [P, STILES])
        wr_sb = sb("wr_sb", [P, E])
        br_sb = sb("br_sb", [P, E])
        bias_rows = sb("bias_rows", [E * HC + E, P])
        weights = [sb(f"weights{f}", [P, E * WSTEP]) for f in range(2)]
        w_qkv = sb("w_qkv", [P, 3 * D])
        w_o = sb("w_o", [P, D])
        bias_cols = sb("bias_cols", [P, E * (HC + 1)])
        w_rows = sb("w_rows", [P, 4, D])
        w8 = sb("w8", [P, 3, DH])
        ident_b = sb("ident_b", [P, P], BF16)
        wview = [w[:, :].rearrange("p (e s) -> p e s", e=E) for w in weights]
        X = sb("X", [P, TILES, D])
        XN = sb("XN", [P, TILES, D])
        arena = sb("arena", [P, PSLOTS * 1024])
        at = [0]

        def carve(shape):
            n = 1
            for x in shape[1:]:
                n *= x
            view = arena[:, at[0]:at[0] + n]
            at[0] += n
            assert at[0] <= PSLOTS * 1024
            if len(shape) == 4:
                return view.rearrange("p (a b c) -> p a b c", a=shape[1], b=shape[2])
            return view.rearrange("p (a b) -> p a b", a=shape[1])

        probs = arena[:, :].rearrange("p (s n) -> p s n", s=PSLOTS)

        stats = sb("stats", [P, GT, 6])
        mv = sb("mv", [P, GT, 2])
        rin = sb("rin", [P, GT])
        rout = sb("rout", [P, GT])
        rtmp = sb("rtmp", [P, GT])
        xt = sb("xt", [P, 2, 512])
        sc = sb("sc", [P, GT, E])
        eq = sb("eq", [P, GT, E])
        oh = [sb(f"oh{k}", [P, GT, E]) for k in range(2)]
        both = sb("both", [P, GT, E])
        s2 = sb("s2", [P, GT, E])
        mx = [sb(f"mx{k}", [P, GT]) for k in range(2)]
        fst = sb("fst", [P, GT])
        diff = sb("diff", [P, GROUPS, GT])
        e2 = sb("e2", [P, GROUPS, GT])
        den = sb("den", [P, GT])
        gate = [sb(f"gate{k}", [P, TILES]) for k in range(2)]
        scan = [sb(f"scan{k}", [P, GT, E]) for k in range(2)]
        total = sb("total", [P, GT, E])
        within = sb("within", [P, GT, E])
        place = sb("place", [P, GT, E])
        cnt_i = sb("cnt_i", [P, 2, E], I32)
        cnt = sb("cnt", [P, 6, E])
        dst_f = sb("dst_f", [P, GT])
        dest = [sb(f"dest{k}", [P, TILES], I32) for k in range(2)]
        over = sb("over", [P, STILES, E])
        owner = sb("owner", [P, STILES])
        w_at = sb("w_at", [P, GROUPS, STILES], I32)

        xs = sb("xs", [P, XSLOTS, SUB, D])
        xst = carve([P, 2, ST])
        wbuf = carve([P, 2, WSTEP])
        hid = carve([P, 2, HC, ST])
        yt = carve([P, 2, ST])
        ys = sb("ys", [P, YSLOTS, SUB, D])
        gat = sb("gat", [P, GSLOTS, D])

        qk_at = [w[:, 0:2 * PAIRS * N // 2].bitcast(BF16).rearrange("p (s h n) -> p s h n", s=2, h=PAIRS)
                 for w in weights]
        qT = [qk_at[1][:, 0, :, :], qk_at[0][:, 0, :, :]]
        kT = [qk_at[1][:, 1, :, :], qk_at[0][:, 1, :, :]]
        zeros = weights[1][:, 0:FILL * D // P]
        V = sb("V", [P, 2, BT, HEADS, VW])
        xa = sb("xa", [P, 2 * P])
        qk = sb("qk", [P, BT, 2 * D])
        sq = sb("sq", [P, 2, 2 * D])
        ss = sb("ss", [P, BT, 2 * HEADS])
        rs = sb("rs", [P, BT, 2 * HEADS])
        rst = sb("rst", [P, BT, 2 * HEADS])
        qh = sb("qh", [P, 2, 2 * D])
        rest = sb("rest", [P, 2 * D])
        stack = sb("stack", [P, 2, 2, HEADS, SLOTS, DH], BF16)
        oT = sb("oT", [P, 2, 512])
        osum = sb("osum", [P, 4, 4])
        att = xt[:, :, :].rearrange("p h (t d) -> p h t d", t=4)
        aT = sb("aT", [P, 2, P])

        att8 = xt[:, :, :].rearrange("p h (t d) -> p (h t) d", t=4)
        reach = sb("reach", [P, 1])
        unbounded = sb("unbounded", [P, 1], I32)
        g_p, g_pt = arena[:, 0:1024], arena[:, 1024:2048]
        g_k = arena[:, 2048:2560].bitcast(BF16)
        g_q = arena[:, 2560:2624].bitcast(BF16)
        g_v = arena[:, 2624:2624 + BT * 2 * VW].rearrange("p (c r v) -> p c r v", c=BT, r=2)
        g_max = arena[:, 3000:3001]

        bounded = sem("bounded")
        attended = sem("attended")
        pool_alink = sem("pool_alink")
        dve_alink = sem("dve_alink")
        rs_ready = sem("rs_ready")
        normalised = sem("normalised")
        g_ready = sem("g_ready")
        g_scores = sem("g_scores")
        g_maxed = sem("g_maxed")
        g_exp = sem("g_exp")
        g_turned = sem("g_turned")
        g_copied = sem("g_copied")
        g_out = sem("g_out")
        g_done = sem("g_done")
        xnorm = sem("xnorm")
        scores_full = sem("scores_full")
        exp_done = sem("exp_done")
        pv_done = sem("pv_done")
        ot_full = sem("ot_full")
        aux_full = sem("aux_full")
        aux_read = sem("aux_read")
        squared = sem("squared")
        summed = sem("summed")
        stacked = sem("stacked")
        w_turned = sem("w_turned")
        w_copied = sem("w_copied")
        a_loaded = sem("a_loaded")
        w_again = sem("w_again")
        x_loaded = [sem(f"x_loaded{g}") for g in range(GROUPS)]
        r_loaded = sem("r_loaded")
        w_loaded = sem("w_loaded")
        b_loaded = sem("b_loaded")
        filled = [sem(f"filled{g}") for g in range(GROUPS)]
        consts = sem("consts")
        pool_link = sem("pool_link")
        dve_link = sem("dve_link")
        bias_t = sem("bias_t")
        bias_in = sem("bias_in")
        xn_ready = sem("xn_ready")
        diff_ready = sem("diff_ready")
        gate_exp = sem("gate_exp")
        r_full = sem("r_full")
        r_read = sem("r_read")
        picks = sem("picks")
        routed = sem("routed")
        scattered = [sem(f"scattered{g}") for g in range(GROUPS)]
        xs_in = [sem(f"xs_in{k}") for k in range(XSLOTS)]
        ys_out = [sem(f"ys_out{k}") for k in range(YSLOTS)]
        g_in = [sem(f"g_in{k}") for k in range(GSLOTS)]
        xs_turned = sem("xs_turned")
        xst_full = sem("xst_full")
        w_full = sem("w_full")
        h_full = sem("h_full")
        relu_done = sem("relu_done")
        y_full = sem("y_full")
        yt_full = sem("yt_full")
        o_full = sem("o_full")
        ys_full = sem("ys_full")
        half_in = sem("half_in")
        combined = sem("combined")
        out_done = sem("out_done")

        LOADS_W = 1 + E
        PEEL = (1, PHASES[1].stiles // 4 - 1, 3, 1)

        def full(pl):
            return r_full if pl is ROUTES else aux_full

        def read(pl):
            return r_read if pl is ROUTES else aux_read

        def turned_rows(n):
            if n in SECOND[0].quads:
                return xs[:, 2 * (n % 2):2 * (n % 2) + 2, :, :].rearrange("p s j d -> p (s j d)")
            return xt[:, n % 2, :]
        FILL0 = FIRST[0].stiles * ST // FILL
        FILLS = [rows // FILL for rows in SROWS]

        block = ctx.enter_context(nc.Block())

        def branch(eng, attend):
            eng.wait_ge(bounded, 1)
            far = eng.value_load(unbounded[0:1, 0:1], min_val=0, max_val=1)
            with eng.If(far > 0):
                attend(GENERAL)
            with eng.Else():
                attend(FAST)

        def sorted_quads(eng, G, step, peel=1):
            quads = G.stiles // 4
            for t in range(4 * peel):
                step(t, t % 4, t == 0, False)
            if peel < quads - 1:
                with eng.Fori(peel, quads - 1) as q:
                    for j in range(4):
                        step(q * 4 + j, j, False, False)
            for j in range(4):
                step(G.stiles - 4 + j, j, False, j == 3)

        @block.sync
        def _(sp):
            xv = x_in.rearrange("b (n p) d -> p (b n) d", p=P)
            def load_x(g):
                cols = FIRST[g].cols
                sp.dma_start(X[:, cols, :], xv[:, cols, :]).then_inc(x_loaded[g], 16)

            def fill(g, chunks, sem):
                for k in chunks:
                    sp.dma_start(xs_dram[g][k * FILL:(k + 1) * FILL, :].rearrange("(n p) d -> p n d", p=P),
                                 zeros[:, :].rearrange("p (n d) -> p n d", d=D)).then_inc(sem, 16)

            def load_weights(f, sem):
                sp.dma_start(wview[f][:, :, 0:HID], w1.rearrange("e d h -> d e h")).then_inc(sem, 16)
                for e in range(E):
                    sp.dma_start(wview[f][:, e, W2_AT:B1_AT].rearrange("p (c d) -> p c d", c=HC),
                                 w2[e].rearrange("(c p) d -> p c d", p=P)).then_inc(sem, 16)

            load_x(0)
            sp.dma_start(wr_sb[:, :], wr).then_inc(r_loaded, 16)
            sp.dma_start(br_sb[:, :], br.rearrange("(a e) -> a e", a=1).to_broadcast([P, E])).then_inc(r_loaded, 16)
            sp.wait_ge(consts, 1)
            fill(0, range(FILL0), filled[0])
            load_x(1)
            sp.dma_start(bias_rows[0:E * HC, :], b1.rearrange("e (c p) -> (e c) p", p=P)).then_inc(b_loaded, 16)
            sp.dma_start(bias_rows[E * HC:, :], b2).then_inc(b_loaded, 16)
            for i, w in enumerate((wq, wk, wv, wo)):
                sp.dma_start(w_rows[:, i, :], w).then_inc(a_loaded, 16)
            for i, w in enumerate((qn, kn)):
                sp.dma_start(w8[:, i, :], w.rearrange("(a d) -> a d", a=1).to_broadcast([P, DH]))\
                    .then_inc(a_loaded, 16)
            load_weights(0, w_loaded)
            fill(1, range(FILLS[1]), filled[1])
            fill(0, range(FILL0, FILLS[0]), filled[1])

            def experts(G):
                f, g, ph, base = G.f, G.g, G.ph, G.base
                if g == 0:
                    sp.wait_ge(scattered[g], G.scattered)

                def load(t, slot, g=g):
                    sp.dma_start(xs[:, slot, :, :],
                                 xs_dram[g][bass.ds(t * ST, ST), :].rearrange("(j p) d -> p j d", p=P))\
                        .then_inc(xs_in[slot], 16)

                if g == 0:
                    for t in range(XSLOTS - 1):
                        if ph:
                            sp.wait_ge(xs_turned, base)
                        load(t, t)

                def step(t, slot, first, last):
                    if not isinstance(t, int) or t + XSLOTS - 1 < G.stiles:
                        if not (ph == 0 and first):
                            sp.wait_ge(xs_turned, t + base)
                        load(t + XSLOTS - 1, (slot + XSLOTS - 1) % XSLOTS)
                    elif g == 0:
                        n = t + XSLOTS - 1 - G.stiles
                        if n == 0:
                            sp.wait_ge(scattered[1], PHASES[ph + 1].scattered)
                        sp.wait_ge(xs_turned, t + base)
                        load(n, n, 1)
                    sp.wait_ge(ys_full, t + (base + 1))
                    sp.dma_start(ys_dram[g][bass.ds(t * ST, ST), :].rearrange("(j p) d -> p j d", p=P),
                                 ys[:, slot % YSLOTS, :, :]).then_inc(ys_out[slot % YSLOTS], 16)

                sorted_quads(sp, G, step)

            for G in FIRST:
                experts(G)

            def reload(pl):
                if pl is FAST:
                    sp.wait_ge(pv_done, 8 * BLOCKS * (BATCH - 1))
                else:
                    sp.wait_ge(attended, 1)
                load_weights(1, w_again)

            branch(sp, reload)
            for G in SECOND:
                experts(G)
            at = 0
            ov = out.rearrange("b (n p) d -> p (b n) d", p=P)
            for to in STORES:
                sp.wait_ge(combined, TILES + to)
                sp.dma_start(ov[:, at:to, :], X[:, at:to, :]).then_inc(out_done, 16)
                at = to
            sp.wait_ge(out_done, 16 * len(STORES))

        @block.gpsimd
        def _(pool):
            link = Link(pool, pool_link)
            pool.memset(zeros[:, :], 0.0).then_inc(consts, 1)
            link(pool.memset(ident[:, :], 0.0))
            pool.affine_select(out=ident[:, :], in_=ident[:, :], compare_op=ALU.not_equal, fill=1.0, base=0,
                               pattern=[[-1, P]], channel_multiplier=1).then_inc(consts, 1)
            link(pool.memset(before[:, :], 0.0))
            pool.affine_select(out=before[:, :], in_=before[:, :], compare_op=ALU.is_ge, fill=1.0, base=0,
                               pattern=[[-1, P]], channel_multiplier=1).then_inc(consts, 1)
            pool.iota(erow_i[:, :], pattern=[[-1, E]], base=E, channel_multiplier=0)
            link(pool.iota(trow_i[:, :], pattern=[[1, STILES]], base=0, channel_multiplier=0))
            pool.tensor_copy(erow[:, :], erow_i[:, :])
            pool.tensor_copy(trow[:, :], trow_i[:, :])
            pool.memset(ones[:, :], 1.0).then_inc(consts, 1)

            def scatter(G):
                g, ph = G.g, G.ph
                if not G.f:
                    pool.wait_ge(filled[G.g], 16 * (FILLS[1] + FILLS[0] - FILL0 if G.g else FILL0))
                pool.wait_ge(routed, ph + 1)
                for i in range(G.start, G.start + G.tiles):
                    for k in range(2):
                        pool.indirect_dma_start(xs_dram[g], bass.IndirectOffsetOnAxis(ap=dest[k][:, i:i + 1], axis=0),
                                                XN[:, i, :], None).then_inc(scattered[g], 16)

            def gather(f, t):
                for G in PHASES:
                    if G.f == f and G.start <= t < G.start + G.tiles:
                        at = ys_dram[G.g][0:G.stiles * ST, :]
                        if t == G.start:
                            for k in range(YSLOTS):
                                pool.wait_ge(ys_out[k], 16 * (G.base + G.stiles) // YSLOTS)
                for k in range(2):
                    n = 2 * (f * TILES + t) + k
                    if n >= GSLOTS:
                        pool.wait_ge(combined, (n - GSLOTS) // 2 + 1)
                    pool.indirect_dma_start(gat[:, n % GSLOTS, :], None, at,
                                            bass.IndirectOffsetOnAxis(ap=dest[k][:, t:t + 1], axis=0))\
                        .then_inc(g_in[n % GSLOTS], 16)

            def square(pl, t):
                pool.wait_ge(aux_read, pl.event["qkv", t] + 1)
                if t >= 2:
                    pool.wait_ge(summed, t - 1)
                pool.tensor_tensor(sq[:, t % 2, :], qk[:, t % BT, :], qk[:, t % BT, :], ALU.mult).then_inc(squared, 1)

            def normalise(t, alink):
                heads = qh[:, t % 2, :].rearrange("p (h d) -> p h d", d=DH)
                keys = heads[:, HEADS:, :]
                pool.wait_ge(rs_ready, t // BT + 1)
                if t >= 2:
                    pool.wait_ge(stacked, t - 1)
                alink(pool.tensor_tensor(heads, qk[:, t % BT, :].rearrange("p (h d) -> p h d", d=DH),
                                         rs[:, t % BT, :].unsqueeze(2).to_broadcast([P, 2 * HEADS, DH]), ALU.mult))
                pool.tensor_tensor(keys, keys, w8[:, 2, :].unsqueeze(1).to_broadcast([P, HEADS, DH]), ALU.mult)\
                    .then_inc(normalised, 1)

            def attend(pl, alink):
                for items in pl.blocks:
                    for kind, n, _ in items:
                        if kind == "sums":
                            square(pl, n)
                        elif kind == "split":
                            normalise(n, alink)
                        elif kind == "gather":
                            gather(0, n)
                        elif kind == "place":
                            scatter(SECOND[0])

            for G in FIRST:
                scatter(G)
            link(pool.memset(V[:, :, :, :, :], 0.0))
            pool.memset(V[:, :, :, :, DH:DH + 1], 1.0).then_inc(consts, 1)
            attend(PREFIX, link)
            branch(pool, lambda pl: attend(pl, Link(pool, pool_alink)))
            scatter(SECOND[1])
            for t in range(TILES):
                gather(1, t)

        @block.vector
        def _(dve):
            link = Link(dve, dve_link)
            alink = Link(dve, dve_alink)

            def rsqrt(dst, src, tmp, link=link):
                link(dve.tensor_scalar(tmp.bitcast(I32), src.bitcast(I32), 1, None, ALU.logical_shift_right))
                link(dve.tensor_scalar(dst.bitcast(I32), tmp.bitcast(I32), -1.0, float(0x5f3759df), ALU.mult, ALU.add))
                for _ in range(3):
                    link(dve.tensor_tensor(tmp, dst, dst, ALU.mult))
                    link(dve.scalar_tensor_tensor(out=tmp, in0=tmp, scalar=-0.5, in1=src, op0=ALU.mult, op1=ALU.mult))
                    link(dve.scalar_tensor_tensor(out=dst, in0=tmp, scalar=1.5, in1=dst, op0=ALU.add, op1=ALU.mult))

            def layer_norm(tiles, ready, link=link):
                n = len(tiles)
                for i, t in enumerate(tiles):
                    last = dve.bn_stats(stats[:, i, :], X[:, t, :])
                link(last)
                for i in range(n):
                    last = dve.bn_aggr(mv[:, i, :], stats[:, i, :])
                link(last)
                link(dve.tensor_scalar(rin[:, 0:n], mv[:, 0:n, 1], EPS_LN, None, ALU.add))
                rsqrt(rout[:, 0:n], rin[:, 0:n], rtmp[:, 0:n], link)
                for i, t in enumerate(tiles):
                    dve.tensor_scalar(XN[:, t, :], X[:, t, :], mv[:, i, 0:1], rout[:, i:i + 1],
                                      ALU.subtract, ALU.mult).then_inc(ready, 1)

            def wide(ap):
                return ap.unsqueeze(2).to_broadcast([P, ap.shape[1], E])

            def norm_routed(f, tiles, link):
                if f:
                    for G in FIRST:
                        dve.wait_ge(scattered[G.g], G.scattered)
                layer_norm(tiles, xn_ready, link)

            def pick(ph, link):
                G = PHASES[ph]
                n = G.tiles
                for k, s in enumerate((sc, s2)):
                    link(dve.tensor_reduce(mx[k][:, 0:n], s[:, 0:n, :], AX.X, ALU.max))
                    link(dve.tensor_tensor(eq[:, 0:n, :], s[:, 0:n, :], wide(mx[k][:, 0:n]), ALU.is_equal))
                    link(dve.tensor_tensor(eq[:, 0:n, :], eq[:, 0:n, :],
                                           erow[:, :].unsqueeze(1).to_broadcast([P, n, E]), ALU.mult))
                    link(dve.tensor_reduce(fst[:, 0:n], eq[:, 0:n, :], AX.X, ALU.max))
                    link(dve.tensor_tensor(oh[k][:, 0:n, :], eq[:, 0:n, :], wide(fst[:, 0:n]), ALU.is_equal))
                    if k == 0:
                        link(dve.scalar_tensor_tensor(out=s2[:, 0:n, :], in0=oh[0][:, 0:n, :], scalar=-BIG,
                                                      in1=sc[:, 0:n, :], op0=ALU.mult, op1=ALU.add))
                dve.tensor_tensor(both[:, 0:n, :], oh[0][:, 0:n, :], oh[1][:, 0:n, :], ALU.add).then_inc(picks, 1)
                dve.tensor_tensor(diff[:, G.g, 0:n], mx[1][:, 0:n], mx[0][:, 0:n], ALU.subtract)\
                    .then_inc(diff_ready, 1)

            def gates(G):
                n = G.tiles
                dve.wait_ge(gate_exp, G.ph + 1)
                link(dve.tensor_scalar(den[:, 0:n], e2[:, G.g, 0:n], 1.0, None, ALU.add))
                link(dve.reciprocal(den[:, 0:n], den[:, 0:n]))
                link(dve.tensor_scalar(gate[0][:, G.cols], den[:, 0:n], 0.5, None, ALU.mult))
                link(dve.tensor_tensor(gate[1][:, G.cols], gate[0][:, G.cols], e2[:, G.g, 0:n], ALU.mult))

            def place_rows(ph, link):
                G = PHASES[ph]
                tiles, stiles = G.tiles, G.stiles
                src, s, k = total, 1, 0
                while s < tiles:
                    dve.tensor_copy(scan[k][:, 0:s, :], src[:, 0:s, :])
                    link(dve.tensor_tensor(scan[k][:, s:tiles, :], src[:, s:tiles, :], src[:, 0:tiles - s, :], ALU.add))
                    src, s, k = scan[k], 2 * s, 1 - k
                dve.tensor_tensor(place[:, 0:tiles, :], src[:, 0:tiles, :], total[:, 0:tiles, :], ALU.subtract)
                link(dve.tensor_scalar(cnt_i[:, 0, :], src[:, tiles - 1, :], float(ST - 1), None, ALU.add))
                link(dve.tensor_scalar(cnt_i[:, 1, :], cnt_i[:, 0, :], ST.bit_length() - 1, None,
                                       ALU.logical_shift_right))
                link(dve.tensor_copy(cnt[:, 0, :], cnt_i[:, 1, :]))
                for n, s in enumerate((1, 2, 4)):
                    dve.tensor_copy(cnt[:, n + 1, 0:s], cnt[:, n, 0:s])
                    link(dve.tensor_tensor(cnt[:, n + 1, s:E], cnt[:, n, s:E], cnt[:, n, 0:E - s], ALU.add))
                link(dve.tensor_tensor(cnt[:, 4, :], cnt[:, 3, :], cnt[:, 0, :], ALU.subtract))
                link(dve.tensor_scalar(cnt[:, 5, :], cnt[:, 4, :], float(ST), None, ALU.mult))
                link(dve.tensor_tensor(place[:, 0:tiles, :], place[:, 0:tiles, :], within[:, 0:tiles, :], ALU.add))
                link(dve.tensor_tensor(place[:, 0:tiles, :], place[:, 0:tiles, :],
                                       cnt[:, 5, :].unsqueeze(1).to_broadcast([P, tiles, E]), ALU.add))
                for k in range(2):
                    link(dve.tensor_tensor(eq[:, 0:tiles, :], oh[k][:, 0:tiles, :], place[:, 0:tiles, :], ALU.mult))
                    link(dve.tensor_reduce(dst_f[:, 0:tiles], eq[:, 0:tiles, :], AX.X, ALU.add))
                    link(dve.tensor_copy(dest[k][:, G.cols], dst_f[:, 0:tiles]))
                link(dve.tensor_tensor(over[:, 0:stiles, :], cnt[:, 3, :].unsqueeze(1).to_broadcast([P, stiles, E]),
                                       trow[:, 0:stiles].unsqueeze(2).to_broadcast([P, stiles, E]), ALU.is_le))
                link(dve.tensor_reduce(owner[:, 0:stiles], over[:, 0:stiles, :], AX.X, ALU.add))
                dve.tensor_scalar(w_at[:, G.g, 0:stiles], owner[:, 0:stiles], float(E - 1), float(WSTEP), ALU.min, ALU.mult)\
                    .then_inc(routed, 1)

            def combine(f, t, j):
                x = X[:, bass.ds(t, 1), :].rearrange("p a d -> p (a d)")
                for k in range(2):
                    dve.wait_ge(g_in[2 * j + k], (t - j) * 4 + 16 * (f * TILES // 4 + 1))
                    ins = dve.scalar_tensor_tensor(out=x, in0=gat[:, 2 * j + k, :],
                                                   scalar=gate[k][:, bass.ds(t, 1)], in1=x,
                                                   op0=ALU.mult, op1=ALU.add)
                    if k == 0:
                        ins.then_inc(half_in, 1)
                        dve.wait_ge(half_in, t + (f * TILES + 1))
                    else:
                        ins.then_inc(combined, 1)

            def experts(G):
                f, g, ph, base = G.f, G.g, G.ph, G.base

                def turned(t, slot):
                    dve.wait_ge(xs_turned, t + (base + 1))
                    dve.tensor_copy(xst[:, slot % 2, :], bank[4][:, 0:ST]).then_inc(xst_full, 1)

                def rows(t, slot):
                    dve.wait_ge(o_full, t + (base + 1))
                    if not isinstance(t, int) or t >= YSLOTS:
                        dve.wait_ge(ys_out[slot % 2], (t - slot % 2) * 8 + 8 * base)
                    elif ph:
                        dve.wait_ge(ys_out[slot % 2], 8 * base)
                    dve.tensor_copy(ys[:, slot % 2, :, :], bank[5][:, 0:ST].rearrange("p (j d) -> p j d", d=D))\
                        .then_inc(ys_full, 1)

                turned(0, 0)

                def step(t, slot, first, last):
                    if not last:
                        turned(t + 1, slot + 1)
                    if not first:
                        rows(t - 1, slot - 1 + 4)
                    if ph == 3 and 3 <= t < 3 + SECOND[0].tiles // 2:
                        for i in range(2 * (t - 3), 2 * (t - 3) + 2):
                            combine(f, i, i % 4)
                    if ph == 1 and t < len(PREFIX.blocks):
                        aside(PREFIX, PREFIX.blocks[t], link)
                    if ph == 2 and first:
                        norm_routed(1, NORMS[4], link)
                    if ph in BESIDE and isinstance(t, int) and t < len(BESIDE[ph]):
                        aside(ROUTES, BESIDE[ph][t], link)

                sorted_quads(dve, G, step, G.stiles // 4 - 1 if ph == 3 else PEEL[ph])
                rows(G.stiles - 1, 3)


            def place_biases(f):
                dve.tensor_copy(wview[f][:, :, B1_AT:B2_AT], bias_cols[:, 0:E * HC].rearrange("p (e c) -> p e c", e=E))
                dve.tensor_copy(wview[f][:, :, B2_AT], bias_cols[:, E * HC:]).then_inc(bias_in, 1)

            def evac_o(pl, K):
                dve.wait_ge(pv_done, 8 * (K + 1))
                if K >= 2:
                    dve.wait_ge(aux_full, pl.event["turn_o", K - 2] + 1)
                dve.tensor_copy(oT[:, K % 2, :], bank[4 + K % 2]).then_inc(ot_full, 1)

            def norm(b, link):
                dve.wait_ge(combined, (b + 1) * BT)
                layer_norm(range(b * BT, (b + 1) * BT), xnorm, link)

            def sums(t):
                dve.wait_ge(squared, t + 1)
                dve.tensor_reduce(ss[:, t % BT, :], sq[:, t % 2, :].rearrange("p (h d) -> p h d", d=DH),
                                  AX.X, ALU.add).then_inc(summed, 1)

            def rsqrt_qk(b, alink):
                dve.wait_ge(summed, (b + 1) * BT)
                alink(dve.tensor_scalar(ss[:, :, :], ss[:, :, :], 1.0 / DH, EPS_RMS, ALU.mult, ALU.add))
                rsqrt(*(a[:, :, :].rearrange("p t h -> p (t h)") for a in (rs, ss, rst)), alink)
                dve.sem_inc(rs_ready, 1)

            def split(pl, t, alink):
                u = t % 2
                dve.wait_ge(normalised, t + 1)
                if t >= 2:
                    dve.wait_ge(aux_full, pl.event["turn_k", t - 2] + 1)
                whole = qh[:, u, :].rearrange("p (a h d) -> p a h d", a=2, d=DH)
                left = rest[:, :].rearrange("p (a h d) -> p a h d", a=2, d=DH)
                first = [stack[:, u, a, :, 0, :] for a in range(2)]
                second = [stack[:, u, 0, :, 3, :], stack[:, u, 1, :, 1, :]]

                def wide(ap, n):
                    return ap.unsqueeze(2).to_broadcast([P, HEADS, n, DH])

                dve.tensor_copy(stack[:, u, 0, :, 0:3, :], wide(whole[:, 0], 3))
                alink(dve.tensor_copy(stack[:, u, 1, :, 0:SLOTS:3, :], wide(whole[:, 1], 3)))
                for a in range(2):
                    last = dve.tensor_tensor(left[:, a], whole[:, a], first[a], ALU.subtract)
                alink(last)
                dve.tensor_copy(stack[:, u, 0, :, 3:6, :], wide(left[:, 0], 3))
                alink(dve.tensor_copy(stack[:, u, 1, :, 1:SLOTS:3, :], wide(left[:, 1], 3)))
                dve.tensor_tensor(stack[:, u, 0, :, 6:8, :], wide(left[:, 0], 2), wide(second[0], 2), ALU.subtract)
                dve.tensor_tensor(stack[:, u, 1, :, 2:SLOTS:3, :], wide(left[:, 1], 2), wide(second[1], 2),
                                  ALU.subtract).then_inc(stacked, 1)

            def empty(pl, kind, n, link):
                src = bank[pl.bank[kind, n]]
                dve.wait_ge(full(pl), pl.event[kind, n] + 1)
                if kind == "turn_x":
                    ins = dve.tensor_copy(xa[:, :], src[:, 0:2 * P])
                elif kind == "qkv":
                    dve.tensor_copy(qk[:, n % BT, :], src[:, 0:2 * D])
                    ins = dve.tensor_copy(V[:, n // BT % 2, n % BT, :, 0:DH],
                                          src[:, 2 * D:3 * D].rearrange("p (h d) -> p h d", d=DH))
                elif kind in ("turn_q", "turn_k"):
                    to = (qT if kind == "turn_q" else kT)[n // BT % 2][:, :, n % BT * P:(n % BT + 1) * P]
                    ins = dve.tensor_scalar(to.bitcast(I32), src.bitcast(I32).rearrange("p (h n) -> p h n", h=PAIRS),
                                            0, None, ALU.logical_shift_right)
                elif kind == "turn_o":
                    half, g = divmod(n, 4)
                    v = src.rearrange("p (t j r) -> p t j r", t=4, j=4)
                    alink(dve.reciprocal(osum[:, :, :], v[:, :, :, DH]))
                    ins = dve.tensor_tensor(
                        att[:, half % 2, :, g * 4 * DH:(g + 1) * 4 * DH].rearrange("p t (j d) -> p t j d", d=DH),
                        v[:, :, :, 0:DH], osum[:, :, :].unsqueeze(3).to_broadcast([P, 4, 4, DH]), ALU.mult)
                elif kind == "turn_a":
                    ins = dve.tensor_copy(aT[:, n % 2, :], src[:, 0:P])
                elif kind == "wo":
                    ins = dve.tensor_tensor(X[:, n, :], src[:, 0:D], X[:, n, :], ALU.add)
                elif kind == "r_turn":
                    if ("router", n - 2) in pl.event:
                        dve.wait_ge(full(pl), pl.event["router", n - 2] + 1)
                    ins = dve.tensor_copy(turned_rows(n), src)
                elif kind == "router":
                    G = next(G for G in PHASES if n in G.quads)
                    q = n - G.quads[0]
                    ins = dve.tensor_tensor(sc[:, 4 * q:4 * q + 4, :],
                                            src[:, 0:4 * E].rearrange("p (t e) -> p t e", e=E),
                                            br_sb[:, :].unsqueeze(1).to_broadcast([P, 4, E]), ALU.add)
                    if n == G.quads[-1]:
                        link(ins)
                        ins = None
                elif kind == "count":
                    k = PHASES[n].tiles
                    dve.tensor_copy(within[:, 0:k, :], src[:, 0:k * E].rearrange("p (t e) -> p t e", e=E))
                    link(dve.tensor_copy(total[:, 0:k, :],
                                         src[:, k * E:2 * k * E].rearrange("p (t e) -> p t e", e=E)))
                    ins = None
                if ins is None:
                    dve.sem_inc(read(pl), 1)
                else:
                    ins.then_inc(read(pl), 1)

            def general(pl, b):
                links, base = 5, alink.at
                dve.wait_ge(aux_read, pl.event["turn_k", (b + 1) * BT - 1] + 1)
                with dve.Fori(0, PAIRS) as pair:
                    with dve.Fori(0, BT) as i:
                        turn = pair * BT + i
                        at = (turn + b * PAIRS * BT) * 2
                        alink.at = turn * links + base
                        dve.tensor_copy(g_k, kT[b % 2][:, bass.ds(pair, 1), :].rearrange("p a n -> p (a n)"))
                        for r in range(2):
                            dve.tensor_copy(g_v[:, :, r, :],
                                            V[:, b % 2, :, bass.ds(pair * 2 + r, 1), :].rearrange("p c a v -> p c (a v)"))
                        alink(dve.tensor_copy(g_q, qT[b % 2][:, bass.ds(pair, 1), bass.ds(i * P, P)]
                                              .rearrange("p a n -> p (a n)")))
                        dve.sem_inc(g_ready, 1)
                        for r in range(2):
                            dve.wait_ge(g_scores, at + (r + 1))
                            dve.tensor_reduce(g_max, psum[:, 0:2, :].rearrange("p b n -> p (b n)"), AX.X, ALU.max,
                                              negate=True).then_inc(g_maxed, 1)
                            dve.wait_ge(g_turned, at + (r + 1))
                            dve.tensor_copy(g_pt, psum[:, 2:4, :].rearrange("p b n -> p (b n)")).then_inc(g_copied, 1)
                            dve.wait_ge(g_out, at + (r + 1))
                            alink(dve.reciprocal(osum[:, 0, 0:1], bank[4][:, DH:DH + 1]))
                            alink(dve.tensor_scalar(
                                att8[:, bass.ds(i, 1), bass.ds(pair * (2 * DH) + r * DH, DH)]
                                .rearrange("p a n -> p (a n)"),
                                bank[4][:, 0:DH], osum[:, 0, 0:1], None, ALU.mult))
                alink.at = base + PAIRS * BT * links
                dve.sem_inc(g_done, 1)

            def aside(pl, items, link):
                for kind, n, step in items:
                    if step is not None:
                        empty(pl, kind, n, link)
                    elif kind == "evac_o":
                        evac_o(pl, n)
                    elif kind == "norm":
                        norm(n, link)
                    elif kind == "sums":
                        sums(n)
                    elif kind == "rsqrt":
                        rsqrt_qk(n, link)
                    elif kind == "split":
                        split(pl, n, link)
                    elif kind == "general":
                        general(pl, n)
                    elif kind == "combine":
                        combine(0, n, n % 4)
                    elif kind == "rnorm":
                        norm_routed(1, NORMS[n], link)
                    elif kind == "pick":
                        pick(n, link)
                    elif kind == "place":
                        place_rows(n, link)

            def attend(pl):
                alink.at = 0
                dve.wait_ge(w_full, SECOND[0].base)
                for items in pl.blocks:
                    aside(pl, items, alink)
                dve.wait_ge(aux_read, len(pl.event))
                dve.sem_inc(attended, 1)

            dve.memset(psum[:, 4:6, :], 0.0)
            dve.wait_ge(r_loaded, 16 * 2)
            for g in range(GROUPS):
                dve.wait_ge(x_loaded[g], 16)
                if g == 0:
                    dve.wait_ge(consts, 4)
                norm_routed(0, range(TILES)[FIRST[g].cols], link)
                aside(ROUTES, ROUTES.blocks[g], link)
            dve.tensor_copy(ident_b[:, :], ident[:, :])
            dve.wait_ge(a_loaded, 16 * 6)
            link(dve.tensor_tensor(w8[:, 2, :], w8[:, 0, :], w8[:, 1, :], ALU.mult))
            link(dve.tensor_scalar(w8[:, 2, :], w8[:, 2, :], SCALE, None, ALU.mult))
            link(dve.tensor_reduce(reach[:, :], w8[:, 2, :], AX.X, ALU.max, apply_absolute_value=True))
            dve.tensor_scalar(unbounded[:, :], reach[:, :], MAX_BOUND / DH, None, ALU.is_gt).then_inc(bounded, 1)
            dve.wait_ge(w_turned, 1)
            dve.tensor_copy(w_qkv[:, :], bank[6][:, 0:3 * D])
            dve.tensor_copy(w_o[:, :], bank[6][:, 3 * D:4 * D]).then_inc(w_copied, 1)
            dve.wait_ge(bias_t, 1)
            link(dve.tensor_copy(bias_cols[:, :], bank[7][:, 0:E * (HC + 1)]))
            place_biases(0)
            experts(FIRST[0])
            gates(FIRST[0])
            dve.wait_ge(consts, 5)
            experts(FIRST[1])
            gates(FIRST[1])
            branch(dve, attend)
            dve.wait_ge(w_again, 16 * (1 + E))
            place_biases(1)
            experts(SECOND[0])
            gates(SECOND[0])
            experts(SECOND[1])
            gates(SECOND[1])
            for t in range(SECOND[1].start, TILES):
                combine(1, t, t % 4)

        @block.scalar
        def _(act):
            def gate(G):
                act.wait_ge(diff_ready, G.ph + 1)
                act.activation(e2[:, G.g, 0:G.tiles], diff[:, G.g, 0:G.tiles], ACT.Exp).then_inc(gate_exp, 1)

            def experts(G):
                f, g, ph, base = G.f, G.g, G.ph, G.base

                def fetch(t, slot):
                    at = act.value_load(w_at[0:1, g, bass.ds(t, 1)], min_val=0, max_val=(E - 1) * WSTEP)
                    if not (ph == 0 and isinstance(t, int) and t < 2):
                        act.wait_ge(yt_full, t + (base - 1))
                    act.activation(wbuf[:, slot % 2, 0:WUSED], weights[f][:, bass.ds(at, WUSED)], ACT.Copy)\
                        .then_inc(w_full, 1)

                act.wait_ge(routed, ph + 1)
                fetch(0, 0)

                def step(t, slot, first, last):
                    for c in range(HC):
                        act.wait_ge(h_full, t * HC + (base * HC + c + 1))
                        act.activation(hid[:, slot % 2, c, :], bank[c][:, 0:ST], ACT.Relu,
                                       bias=wbuf[:, slot % 2, B1_AT + c:B1_AT + c + 1]).then_inc(relu_done, 1)
                    if not last:
                        fetch(t + 1, slot + 1)
                    act.wait_ge(y_full, t + (base + 1))
                    act.activation(yt[:, slot % 2, :], bank[6][:, 0:ST], ACT.Identity,
                                   bias=wbuf[:, slot % 2, B2_AT:B2_AT + 1]).then_inc(yt_full, 1)

                sorted_quads(act, G, step)

            def attend(pl):
                if pl is GENERAL:
                    with act.Fori(0, NB * 2 * BT) as n:
                        act.wait_ge(g_maxed, n + 1)
                        act.activation(g_p, psum[:, 0:2, :].rearrange("p b n -> p (b n)"), ACT.Exp,
                                       bias=g_max).then_inc(g_exp, 1)
                    return

                def block(K):
                    for u in range(16):
                        act.wait_ge(scores_full, K * 16 + (u + 1))
                        if u >= PSLOTS or not isinstance(K, int):
                            act.wait_ge(pv_done, K * 8 + (u // 2 + 1 - PSLOTS // 2))
                        act.activation(probs[:, u % PSLOTS, :],
                                       psum[:, 2 * (u % 2):2 * (u % 2) + 2, :].rearrange("p b n -> p (b n)"),
                                       ACT.Exp).then_inc(exp_done, 1)

                block(0)
                with act.Fori(1, NB) as K:
                    block(K)

            act.wait_ge(w_loaded, 16 * LOADS_W)
            act.wait_ge(bias_in, 1)
            for G in FIRST:
                gate(G)
                experts(G)
            branch(act, attend)
            act.wait_ge(bias_in, 2)
            for G in SECOND:
                gate(G)
                experts(G)

        @block.tensor
        def _(pe):
            def experts(G):
                f, g, ph, base = G.f, G.g, G.ph, G.base

                def turn(t, slot, first=False):
                    pe.wait_ge(xs_in[slot % XSLOTS], (t - slot % XSLOTS) * 4 + (4 * base + 16))
                    if not (ph == 0 and first):
                        pe.wait_ge(xst_full, t + base)
                    for j in range(SUB):
                        mm = pe.transpose(bank[4][:, j * P:(j + 1) * P], xs[:, slot % XSLOTS, j, :], ident[:, :])
                    mm.then_inc(xs_turned, 1)

                def back(t, slot, first=False):
                    pe.wait_ge(yt_full, t + (base + 1))
                    if not (ph == 0 and first):
                        pe.wait_ge(ys_full, t + base)
                    for j in range(SUB):
                        mm = pe.transpose(bank[5][:, j * P:(j + 1) * P], yt[:, slot % 2, j * P:(j + 1) * P],
                                          ident[:, :])
                    mm.then_inc(o_full, 1)

                turn(0, 0, True)

                def step(t, slot, first, last):
                    if not last:
                        turn(t + 1, slot + 1)
                    pe.wait_ge(xst_full, t + (base + 1))
                    pe.wait_ge(w_full, t + (base + 1))
                    for c in range(HC):
                        pe.matmul(bank[c][:, 0:ST], wbuf[:, slot % 2, c * P:(c + 1) * P], xst[:, slot % 2, :],
                                  start=True, stop=True).then_inc(h_full, 1)
                    if not first:
                        back(t - 1, slot - 1 + 4, isinstance(t, int) and t == 1)
                    if ph in BESIDE and first:
                        if ph:
                            pe.wait_ge(attended, 1)
                        else:
                            pe.wait_ge(bias_in, 1)
                    if ph in BESIDE and isinstance(t, int) and t < len(BESIDE[ph]):
                        fills(ROUTES, BESIDE[ph][t])
                    if ph == 1 and t < len(PREFIX.blocks):
                        fills(PREFIX, PREFIX.blocks[t], 0)
                    for c in range(HC):
                        pe.wait_ge(relu_done, t * HC + (base * HC + c + 1))
                        mm = pe.matmul(bank[6][:, 0:ST], wbuf[:, slot % 2, W2_AT + c * D:W2_AT + (c + 1) * D],
                                       hid[:, slot % 2, c, :], start=(c == 0), stop=(c == HC - 1))
                    mm.then_inc(y_full, 1)
                    if ph == 1 and t < len(PREFIX.blocks):
                        fills(PREFIX, PREFIX.blocks[t], 1)

                sorted_quads(pe, G, step, PEEL[ph])
                back(G.stiles - 1, 3)

            def fill(pl, kind, n):
                former = pl.former[kind, n]
                dst = bank[pl.bank[kind, n]]
                if former is not None:
                    pe.wait_ge(read(pl), former + 1)
                if kind == "turn_x":
                    for j in range(2):
                        pe.wait_ge(xnorm, n + j + 1)
                        mm = pe.transpose(dst[:, j * P:(j + 1) * P], XN[:, n + j, :], ident[:, :])
                elif kind == "qkv":
                    pe.wait_ge(aux_read, pl.event["turn_x", n - n % 2] + 1)
                    mm = pe.matmul(dst[:, 0:3 * D], xa[:, n % 2 * P:(n % 2 + 1) * P], w_qkv[:, :],
                                   start=True, stop=True)
                elif kind in ("turn_q", "turn_k"):
                    pe.wait_ge(stacked, n + 1)
                    flat = stack[:, n % 2, int(kind == "turn_k"), :, :, :].rearrange("p h s d -> p (h s d)")
                    for j in range(PAIRS):
                        mm = pe.transpose(dst.bitcast(BF16)[:, j * P:(j + 1) * P], flat[:, j * P:(j + 1) * P],
                                          ident_b[:, :])
                elif kind == "turn_o":
                    pe.wait_ge(ot_full, n + 1)
                    for j in range(4):
                        mm = pe.transpose(dst[:, j * P:(j + 1) * P], oT[:, n % 2, j * P:(j + 1) * P], ident[:, :])
                elif kind == "turn_a":
                    if pl is FAST:
                        pe.wait_ge(aux_read, pl.event["turn_o", n - n % 4 + 3] + 1)
                    else:
                        pe.wait_ge(g_done, n // BT + 1)
                    mm = pe.transpose(dst[:, 0:P], att8[:, n % 8, :], ident[:, :])
                elif kind == "wo":
                    pe.wait_ge(aux_read, pl.event["turn_a", n] + 1)
                    mm = pe.matmul(dst[:, 0:D], aT[:, n % 2, :], w_o[:, :], start=True, stop=True)
                elif kind == "r_turn":
                    for j in range(4):
                        pe.wait_ge(xn_ready, 4 * n + j + 1)
                        mm = pe.transpose(dst[:, j * P:(j + 1) * P], XN[:, (4 * n + j) % TILES, :], ident[:, :])
                elif kind == "router":
                    pe.wait_ge(read(pl), pl.event["r_turn", n] + 1)
                    rows = turned_rows(n)
                    for j in range(4):
                        mm = pe.matmul(dst[:, j * E:(j + 1) * E], rows[:, j * P:(j + 1) * P], wr_sb[:, :],
                                       start=True, stop=True)
                elif kind == "count":
                    pe.wait_ge(picks, n + 1)
                    k = PHASES[n].tiles
                    flat = both[:, 0:k, :].rearrange("p t e -> p (t e)")
                    pe.matmul(dst[:, 0:k * E], before[:, :], flat, start=True, stop=True)
                    mm = pe.matmul(dst[:, k * E:2 * k * E], ones[:, :], flat, start=True, stop=True)
                mm.then_inc(full(pl), 1)

            def scores(K, c, a):
                b, k = divmod(K, BLOCKS)
                half, g = divmod(k, 4)
                u = 16 * K + 2 * c + a
                pair = 2 * g + a
                if u >= 2:
                    pe.wait_ge(exp_done, u - 1)
                for r in range(2):
                    rows = slice(r * KROWS, (r + 1) * KROWS)
                    mm = pe.matmul(bank[2 * a + r], kT[b % 2][rows, pair, c * P:(c + 1) * P],
                                   qT[b % 2][rows, pair, half * 512:(half + 1) * 512], start=True, stop=True)
                mm.then_inc(scores_full, 1)

            def values(K, c):
                b, k = divmod(K, BLOCKS)
                g = k % 4
                if c == 0 and K >= 2:
                    pe.wait_ge(ot_full, K - 1)
                elif c == 0:
                    pe.wait_ge(ys_full, SECOND[0].base)
                pe.wait_ge(exp_done, 16 * K + 2 * c + 2)
                for j in range(4):
                    u = 2 * c + j // 2
                    mm = pe.matmul(bank[4 + K % 2][32 * j:32 * j + VW, :], V[:, b % 2, c, 4 * g + j, :],
                                   probs[:, u % PSLOTS, j % 2 * 512:(j % 2 + 1) * 512],
                                   start=(c == 0), stop=(c == BT - 1))
                mm.then_inc(pv_done, 1)

            def fills(pl, block, at=None):
                for kind, n, step in block:
                    if step is not None and (at is None or step == at):
                        fill(pl, kind, n)

            def general(b):
                with pe.Fori(0, PAIRS * BT) as i:
                    turn = i + b * PAIRS * BT
                    pe.wait_ge(g_ready, turn + 1)
                    for r in range(2):
                        n = turn * 2 + (r + 1)
                        rows = slice(r * KROWS, (r + 1) * KROWS)
                        for h in range(2):
                            mm = pe.matmul(bank[h], g_q[rows, :], g_k[rows, h * 512:(h + 1) * 512],
                                           start=True, stop=True)
                        mm.then_inc(g_scores, 1)
                        pe.wait_ge(g_exp, n)
                        for c in range(BT):
                            mm = pe.transpose(bank[2 + c // 4][:, c % 4 * P:(c % 4 + 1) * P],
                                              g_p[:, c * P:(c + 1) * P], ident[:, :])
                        mm.then_inc(g_turned, 1)
                        pe.wait_ge(g_copied, n)
                        for c in range(BT):
                            mm = pe.matmul(bank[4][:, 0:VW], g_pt[:, c * P:(c + 1) * P], g_v[:, c, r, :],
                                           start=(c == 0), stop=(c == BT - 1))
                        mm.then_inc(g_out, 1)

            def attend(pl):
                if pl is GENERAL:
                    for items in pl.blocks:
                        for kind, n, step in items:
                            if kind == "general":
                                general(n)
                            elif step is not None:
                                fill(pl, kind, n)
                    return
                fills(pl, pl.blocks[0])
                LAG = 2
                for K in range(NB):
                    k = K % BLOCKS
                    if k == 0 and K:
                        pe.wait_ge(aux_read, pl.event["turn_k", (K // BLOCKS + 1) * BT - 1] + 1)
                    for c in range(BT):
                        if K == 0:
                            pe.wait_ge(aux_read, pl.event["turn_k", max(c, EARLY - 1)] + 1)
                        scores(K, c, 0)
                        s = BT * K + c - LAG
                        if s >= 0:
                            values(s // BT, s % BT)
                        scores(K, c, 1)
                        fills(pl, pl.blocks[K + 1], c)
                    if K == NB - 1:
                        for c in range(BT - LAG, BT):
                            values(K, c)
                for K in range(NB, NB + 4):
                    fills(pl, pl.blocks[K + 1])

            pe.wait_ge(consts, 4)
            pe.wait_ge(r_loaded, 16 * 2)
            for g in range(GROUPS):
                fills(ROUTES, ROUTES.blocks[g])
            pe.wait_ge(a_loaded, 16 * 6)
            for i in range(4):
                mm = pe.transpose(bank[6][:, i * D:(i + 1) * D], w_rows[:, i, :], ident[:, :])
            mm.then_inc(w_turned, 1)
            pe.wait_ge(b_loaded, 32)
            pe.transpose(bank[7][:, 0:E * HC + E], bias_rows[:, :], ident[0:E * HC + E, 0:E * HC + E])\
                .then_inc(bias_t, 1)
            pe.wait_ge(w_copied, 1)
            for G in FIRST:
                experts(G)
            pe.wait_ge(aux_read, len(PREFIX.event))
            for _ in range(8):
                pe.matmul(bank[7][:, 0:P], ident[:, :], ident[:, :], start=True, stop=True)
            branch(pe, attend)
            for G in SECOND:
                experts(G)


_INS = ['L0_attn_x', 'L0_attn_Wq', 'L0_attn_Wk', 'L0_attn_Wv', 'L0_attn_Wo', 'L0_attn_qn_w', 'L0_attn_kn_w',
        'L0_ffn_Wr', 'L0_ffn_br', 'L0_ffn_W1', 'L0_ffn_b1', 'L0_ffn_W2', 'L0_ffn_b2']


def kernel(**inputs):
    import numpy as _np
    import concourse.bacc as _bacc
    from concourse import mybir as _mybir
    from concourse.bass_utils import run_bass_kernel_spmd as _run

    nc = _bacc.Bacc("TRN2", target_bir_lowering=False, num_devices=1)
    arrays, args = {}, []
    for name in _INS:
        a = _np.ascontiguousarray(inputs[name])
        arrays[f"in_{name}_dram"] = a
        args.append(nc.dram_tensor(f"in_{name}_dram", a.shape, _mybir.dt.from_np(a.dtype), kind="ExternalInput").ap())
    out = nc.dram_tensor("out_0_dram", (BATCH, N, D), F32, kind="ExternalOutput").ap()
    build(nc, *args, out)
    r = _run(nc, [arrays], core_ids=[0])
    return r.results[0]["out_0_dram"]
```
